# Optimizing a Trainium2 kernel written in Bass

```python
import numpy as np
import jax
import jax.numpy as jnp

def _softmax(x, axis=-1):
    return jax.nn.softmax(x, axis=axis)

def _gelu(x):
    return jax.nn.gelu(x, approximate=True)

def _silu(x):
    return jax.nn.silu(x)

def _sigmoid(x):
    return jax.nn.sigmoid(x)

def _layernorm(x, axis=-1, eps=1e-05):
    m = jnp.mean(x, axis=axis, keepdims=True)
    v = jnp.var(x, axis=axis, keepdims=True)
    return (x - m) / jnp.sqrt(v + eps)

def _scatter_add(tgt, idx, src, axis=0):
    return tgt.at[idx].add(src)

def _segment_sum(src, seg, n):
    return jax.ops.segment_sum(src, seg, n)
kernel_name = 'mk_dlrm_tower_d1_rec_r8_4de1dd'

def setup_inputs(seed: int=0):
    np.random.seed(seed)
    _w = jnp.asarray

    def _rec_inputs():
        import jax
        import jax.numpy as jnp
        _tk = jax.random.key(seed)
        dense_ctx = jax.random.normal(jax.random.fold_in(_tk, 190), (1024, 16), jnp.float32)
        ids = jnp.stack([jax.random.randint(jax.random.fold_in(_tk, 200 + f), (1024,), 0, v, jnp.int32) for f, v in enumerate([1000, 125000, 12500, 12500, 125000, 1250, 1000, 12500, 12500, 125000, 125000, 12500, 1000, 1250, 1000, 125000, 125000, 1250, 12500, 12500, 1250, 1250, 1250, 12500, 1250, 125000, 125000, 125000, 12500, 1250, 12500, 125000, 1000, 1000, 1250, 12500, 125000, 125000, 1000])], axis=1)
        tbl_0 = 0.05 * jax.random.normal(jax.random.fold_in(_tk, 500 + 0), (1000, 16), jnp.float32)
        tbl_1 = 0.05 * jax.random.normal(jax.random.fold_in(_tk, 500 + 1), (125000, 16), jnp.float32)
        tbl_2 = 0.05 * jax.random.normal(jax.random.fold_in(_tk, 500 + 2), (12500, 16), jnp.float32)
        tbl_3 = 0.05 * jax.random.normal(jax.random.fold_in(_tk, 500 + 3), (12500, 16), jnp.float32)
        tbl_4 = 0.05 * jax.random.normal(jax.random.fold_in(_tk, 500 + 4), (125000, 16), jnp.float32)
        tbl_5 = 0.05 * jax.random.normal(jax.random.fold_in(_tk, 500 + 5), (1250, 16), jnp.float32)
        tbl_6 = 0.05 * jax.random.normal(jax.random.fold_in(_tk, 500 + 6), (1000, 16), jnp.float32)
        tbl_7 = 0.05 * jax.random.normal(jax.random.fold_in(_tk, 500 + 7), (12500, 16), jnp.float32)
        tbl_8 = 0.05 * jax.random.normal(jax.random.fold_in(_tk, 500 + 8), (12500, 16), jnp.float32)
        tbl_9 = 0.05 * jax.random.normal(jax.random.fold_in(_tk, 500 + 9), (125000, 16), jnp.float32)
        tbl_10 = 0.05 * jax.random.normal(jax.random.fold_in(_tk, 500 + 10), (125000, 16), jnp.float32)
        tbl_11 = 0.05 * jax.random.normal(jax.random.fold_in(_tk, 500 + 11), (12500, 16), jnp.float32)
        tbl_12 = 0.05 * jax.random.normal(jax.random.fold_in(_tk, 500 + 12), (1000, 16), jnp.float32)
        tbl_13 = 0.05 * jax.random.normal(jax.random.fold_in(_tk, 500 + 13), (1250, 16), jnp.float32)
        tbl_14 = 0.05 * jax.random.normal(jax.random.fold_in(_tk, 500 + 14), (1000, 16), jnp.float32)
        tbl_15 = 0.05 * jax.random.normal(jax.random.fold_in(_tk, 500 + 15), (125000, 16), jnp.float32)
        tbl_16 = 0.05 * jax.random.normal(jax.random.fold_in(_tk, 500 + 16), (125000, 16), jnp.float32)
        tbl_17 = 0.05 * jax.random.normal(jax.random.fold_in(_tk, 500 + 17), (1250, 16), jnp.float32)
        tbl_18 = 0.05 * jax.random.normal(jax.random.fold_in(_tk, 500 + 18), (12500, 16), jnp.float32)
        tbl_19 = 0.05 * jax.random.normal(jax.random.fold_in(_tk, 500 + 19), (12500, 16), jnp.float32)
        tbl_20 = 0.05 * jax.random.normal(jax.random.fold_in(_tk, 500 + 20), (1250, 16), jnp.float32)
        tbl_21 = 0.05 * jax.random.normal(jax.random.fold_in(_tk, 500 + 21), (1250, 16), jnp.float32)
        tbl_22 = 0.05 * jax.random.normal(jax.random.fold_in(_tk, 500 + 22), (1250, 16), jnp.float32)
        tbl_23 = 0.05 * jax.random.normal(jax.random.fold_in(_tk, 500 + 23), (12500, 16), jnp.float32)
        tbl_24 = 0.05 * jax.random.normal(jax.random.fold_in(_tk, 500 + 24), (1250, 16), jnp.float32)
        tbl_25 = 0.05 * jax.random.normal(jax.random.fold_in(_tk, 500 + 25), (125000, 16), jnp.float32)
        tbl_26 = 0.05 * jax.random.normal(jax.random.fold_in(_tk, 500 + 26), (125000, 16), jnp.float32)
        tbl_27 = 0.05 * jax.random.normal(jax.random.fold_in(_tk, 500 + 27), (125000, 16), jnp.float32)
        tbl_28 = 0.05 * jax.random.normal(jax.random.fold_in(_tk, 500 + 28), (12500, 16), jnp.float32)
        tbl_29 = 0.05 * jax.random.normal(jax.random.fold_in(_tk, 500 + 29), (1250, 16), jnp.float32)
        tbl_30 = 0.05 * jax.random.normal(jax.random.fold_in(_tk, 500 + 30), (12500, 16), jnp.float32)
        tbl_31 = 0.05 * jax.random.normal(jax.random.fold_in(_tk, 500 + 31), (125000, 16), jnp.float32)
        tbl_32 = 0.05 * jax.random.normal(jax.random.fold_in(_tk, 500 + 32), (1000, 16), jnp.float32)
        tbl_33 = 0.05 * jax.random.normal(jax.random.fold_in(_tk, 500 + 33), (1000, 16), jnp.float32)
        tbl_34 = 0.05 * jax.random.normal(jax.random.fold_in(_tk, 500 + 34), (1250, 16), jnp.float32)
        tbl_35 = 0.05 * jax.random.normal(jax.random.fold_in(_tk, 500 + 35), (12500, 16), jnp.float32)
        tbl_36 = 0.05 * jax.random.normal(jax.random.fold_in(_tk, 500 + 36), (125000, 16), jnp.float32)
        tbl_37 = 0.05 * jax.random.normal(jax.random.fold_in(_tk, 500 + 37), (125000, 16), jnp.float32)
        tbl_38 = 0.05 * jax.random.normal(jax.random.fold_in(_tk, 500 + 38), (1000, 16), jnp.float32)
        _rk = jax.random.fold_in(_tk, 7)
        W_top1 = 0.0606339 * jax.random.normal(jax.random.fold_in(_tk, 801), (272, 512), jnp.float32)
        W_top2 = 0.0441942 * jax.random.normal(jax.random.fold_in(_tk, 802), (512, 256), jnp.float32)
        W_top3 = 0.0625 * jax.random.normal(jax.random.fold_in(_tk, 803), (256, 1), jnp.float32)
        b_top1 = jnp.zeros((512,), jnp.float32)
        b_top2 = jnp.zeros((256,), jnp.float32)
        return (dense_ctx, ids, tbl_0, tbl_1, tbl_2, tbl_3, tbl_4, tbl_5, tbl_6, tbl_7, tbl_8, tbl_9, tbl_10, tbl_11, tbl_12, tbl_13, tbl_14, tbl_15, tbl_16, tbl_17, tbl_18, tbl_19, tbl_20, tbl_21, tbl_22, tbl_23, tbl_24, tbl_25, tbl_26, tbl_27, tbl_28, tbl_29, tbl_30, tbl_31, tbl_32, tbl_33, tbl_34, tbl_35, tbl_36, tbl_37, tbl_38, W_top1, b_top1, W_top2, b_top2, W_top3)
    dense_ctx, ids, tbl_0, tbl_1, tbl_2, tbl_3, tbl_4, tbl_5, tbl_6, tbl_7, tbl_8, tbl_9, tbl_10, tbl_11, tbl_12, tbl_13, tbl_14, tbl_15, tbl_16, tbl_17, tbl_18, tbl_19, tbl_20, tbl_21, tbl_22, tbl_23, tbl_24, tbl_25, tbl_26, tbl_27, tbl_28, tbl_29, tbl_30, tbl_31, tbl_32, tbl_33, tbl_34, tbl_35, tbl_36, tbl_37, tbl_38, W_top1, b_top1, W_top2, b_top2, W_top3 = _rec_inputs()

    def _L0_rec_setup():
        import jax, jax.numpy as jnp
        import numpy as np
        NUM_FIELD = 39
        CIN_SIZE = [128, 128]
        EMBED_DIM = 16
        BATCH = 256
        key = jax.random.key(seed)
        k1, k2, k3 = jax.random.split(key, 3)
        x_emb = jax.random.normal(k1, (BATCH, NUM_FIELD, EMBED_DIM), dtype=jnp.float32)
        W0 = jax.random.normal(k2, (CIN_SIZE[0], NUM_FIELD * NUM_FIELD), dtype=jnp.float32) * 0.02
        W1 = jax.random.normal(k3, (CIN_SIZE[1], CIN_SIZE[0] * NUM_FIELD), dtype=jnp.float32) * 0.02
        return {'x_emb': x_emb, 'W0': W0, 'W1': W1}
    _L0_rec_all = _L0_rec_setup()
    _L0_rec_in = {k: v for k, v in _L0_rec_all.items() if k in ('W0', 'W1')}
    del _L0_rec_all
    return {'dense_ctx': dense_ctx, 'ids': ids, 'tbl_0': tbl_0, 'tbl_1': tbl_1, 'tbl_2': tbl_2, 'tbl_3': tbl_3, 'tbl_4': tbl_4, 'tbl_5': tbl_5, 'tbl_6': tbl_6, 'tbl_7': tbl_7, 'tbl_8': tbl_8, 'tbl_9': tbl_9, 'tbl_10': tbl_10, 'tbl_11': tbl_11, 'tbl_12': tbl_12, 'tbl_13': tbl_13, 'tbl_14': tbl_14, 'tbl_15': tbl_15, 'tbl_16': tbl_16, 'tbl_17': tbl_17, 'tbl_18': tbl_18, 'tbl_19': tbl_19, 'tbl_20': tbl_20, 'tbl_21': tbl_21, 'tbl_22': tbl_22, 'tbl_23': tbl_23, 'tbl_24': tbl_24, 'tbl_25': tbl_25, 'tbl_26': tbl_26, 'tbl_27': tbl_27, 'tbl_28': tbl_28, 'tbl_29': tbl_29, 'tbl_30': tbl_30, 'tbl_31': tbl_31, 'tbl_32': tbl_32, 'tbl_33': tbl_33, 'tbl_34': tbl_34, 'tbl_35': tbl_35, 'tbl_36': tbl_36, 'tbl_37': tbl_37, 'tbl_38': tbl_38, 'W_top1': W_top1, 'b_top1': b_top1, 'W_top2': W_top2, 'b_top2': b_top2, 'W_top3': W_top3, 'L0_rec_W0': _L0_rec_in['W0'], 'L0_rec_W1': _L0_rec_in['W1']}

def reference(dense_ctx, ids, tbl_0, tbl_1, tbl_2, tbl_3, tbl_4, tbl_5, tbl_6, tbl_7, tbl_8, tbl_9, tbl_10, tbl_11, tbl_12, tbl_13, tbl_14, tbl_15, tbl_16, tbl_17, tbl_18, tbl_19, tbl_20, tbl_21, tbl_22, tbl_23, tbl_24, tbl_25, tbl_26, tbl_27, tbl_28, tbl_29, tbl_30, tbl_31, tbl_32, tbl_33, tbl_34, tbl_35, tbl_36, tbl_37, tbl_38, W_top1, b_top1, W_top2, b_top2, W_top3, L0_rec_W0, L0_rec_W1):
    import jax
    import jax.numpy as jnp

    def _L0_rec_ref(x_emb, W0, W1):
        import jax, jax.numpy as jnp
        import numpy as np
        NUM_FIELD = 39
        CIN_SIZE = [128, 128]
        EMBED_DIM = 16
        BATCH = 256
        B, F, D = x_emb.shape
        x = x_emb
        outs = []
        for W in (W0, W1):
            last = x.shape[1]
            inter = (x[:, :, None, :] * x_emb[:, None, :, :]).reshape(B, last * F, D)
            x = jnp.einsum('bid,hi->bhd', inter, W)
            outs.append(x.sum(axis=-1))
        return jnp.concatenate(outs, axis=-1)
    e = jnp.stack([tbl_0[ids[:, 0]], tbl_1[ids[:, 1]], tbl_2[ids[:, 2]], tbl_3[ids[:, 3]], tbl_4[ids[:, 4]], tbl_5[ids[:, 5]], tbl_6[ids[:, 6]], tbl_7[ids[:, 7]], tbl_8[ids[:, 8]], tbl_9[ids[:, 9]], tbl_10[ids[:, 10]], tbl_11[ids[:, 11]], tbl_12[ids[:, 12]], tbl_13[ids[:, 13]], tbl_14[ids[:, 14]], tbl_15[ids[:, 15]], tbl_16[ids[:, 16]], tbl_17[ids[:, 17]], tbl_18[ids[:, 18]], tbl_19[ids[:, 19]], tbl_20[ids[:, 20]], tbl_21[ids[:, 21]], tbl_22[ids[:, 22]], tbl_23[ids[:, 23]], tbl_24[ids[:, 24]], tbl_25[ids[:, 25]], tbl_26[ids[:, 26]], tbl_27[ids[:, 27]], tbl_28[ids[:, 28]], tbl_29[ids[:, 29]], tbl_30[ids[:, 30]], tbl_31[ids[:, 31]], tbl_32[ids[:, 32]], tbl_33[ids[:, 33]], tbl_34[ids[:, 34]], tbl_35[ids[:, 35]], tbl_36[ids[:, 36]], tbl_37[ids[:, 37]], tbl_38[ids[:, 38]]], axis=1)
    z = _L0_rec_ref(e, L0_rec_W0, L0_rec_W1)
    z = z.reshape(z.shape[0], -1)
    h = jnp.concatenate([z, dense_ctx], axis=1)
    h = jnp.maximum(h @ W_top1 + b_top1, 0.0)
    h = jnp.maximum(h @ W_top2 + b_top2, 0.0)
    y = h @ W_top3
    return y

_drawn_inputs = setup_inputs


def setup_inputs(seed=0):
    import zlib

    import numpy as np

    out = dict(_drawn_inputs(seed))
    spreads = {'b_top1': (0.0, 0.1), 'b_top2': (0.0, 0.1)}
    factors = {'tbl_0': 8.0,
     'tbl_1': 8.0,
     'tbl_2': 8.0,
     'tbl_3': 8.0,
     'tbl_4': 8.0,
     'tbl_5': 8.0,
     'tbl_6': 8.0,
     'tbl_7': 8.0,
     'tbl_8': 8.0,
     'tbl_9': 8.0,
     'tbl_10': 8.0,
     'tbl_11': 8.0,
     'tbl_12': 8.0,
     'tbl_13': 8.0,
     'tbl_14': 8.0,
     'tbl_15': 8.0,
     'tbl_16': 8.0,
     'tbl_17': 8.0,
     'tbl_18': 8.0,
     'tbl_19': 8.0,
     'tbl_20': 8.0,
     'tbl_21': 8.0,
     'tbl_22': 8.0,
     'tbl_23': 8.0,
     'tbl_24': 8.0,
     'tbl_25': 8.0,
     'tbl_26': 8.0,
     'tbl_27': 8.0,
     'tbl_28': 8.0,
     'tbl_29': 8.0,
     'tbl_30': 8.0,
     'tbl_31': 8.0,
     'tbl_32': 8.0,
     'tbl_33': 8.0,
     'tbl_34': 8.0,
     'tbl_35': 8.0,
     'tbl_36': 8.0,
     'tbl_37': 8.0,
     'tbl_38': 8.0,
     'L0_rec_W1': 8.0}
    for name, (base, spread) in spreads.items():
        noise = np.random.default_rng([zlib.crc32(name.encode()), seed]).standard_normal(out[name].shape)
        drawn = base * np.exp(spread * noise) if base else spread * noise
        out[name] = jnp.asarray(drawn.astype(out[name].dtype))
    for name, factor in factors.items():
        out[name] = (out[name] * factor).astype(out[name].dtype)
    return out
```

```python
from contextlib import ExitStack

import concourse.bass as bass
from concourse import mybir

F32 = mybir.dt.float32
BF16 = mybir.dt.bfloat16
I32 = mybir.dt.int32
ALU = mybir.AluOpType
ACT = mybir.ActivationFunctionType

P = 128
FIELDS = 39
WIDTH = 16
BATCH = 1024
TILES = BATCH // P
CHUNKS = 4
CB = P // CHUNKS
COLS = WIDTH * CB
BLOCKS = 4
BB = CB // BLOCKS
PARTS = 3
R = 3
GROUPS = 7
PAIRS = R * FIELDS
GROUP_ROWS = [PAIRS] * 6 + [2 * FIELDS]
ITEMS = 1 + GROUPS
PF = PARTS * FIELDS
J = FIELDS + 1
H = 128
HID1, HID2 = 512, 256
M1, M2 = HID1 // P, HID2 // P
HALF = WIDTH // 2

C_PICK = 0
C_SPREAD = C_PICK + ITEMS * PAIRS
C_IDENT = C_SPREAD + J
C_MASK = C_IDENT + P
C_ALL = C_MASK + BB


def build(nc, ids, tables, consts, w0a, w0b, w1, dense, wt1, wtd, b1, wt2, b2, wt3, out):
    with ExitStack() as ctx:
        def sb(name, shape, dt=F32):
            return ctx.enter_context(nc.sbuf_tensor(name, shape, dt))

        def pb(name):
            return ctx.enter_context(nc.psum_tensor(name, [P, 512], F32))

        def sem(name):
            return ctx.enter_context(nc.semaphore(name))

        ids_sb = sb("ids_sb", [P, TILES, FIELDS], I32)
        rows_now = sb("rows_now", [P, FIELDS], I32)
        consts_sb = sb("consts_sb", [P, C_ALL])
        consts_bf = sb("consts_bf", [P, C_MASK], BF16)
        emb = sb("emb", [P, FIELDS, WIDTH])
        rest = sb("rest", [P, FIELDS, WIDTH])
        parts = sb("parts", [P, PARTS, FIELDS, WIDTH], BF16)
        cols = sb("cols", [P, P, WIDTH], BF16)
        left = sb("left", [P, COLS])
        pairs = sb("pairs", [P, 2, GROUPS, COLS])
        w0 = sb("w0", [P, GROUPS, H])
        w0_other = sb("w0_other", [P, GROUPS, H])
        w1_sb = sb("w1_sb", [P, FIELDS, H])
        spread_e = sb("spread_e", [P, 2, BLOCKS, J, BB])
        x1_sb = sb("x1_sb", [P, BLOCKS, H])
        gram = sb("gram", [P, J, P])
        z2_sb = sb("z2_sb", [P, P])
        dense_sb = sb("dense_sb", [WIDTH, BATCH])
        wtd_sb = sb("wtd_sb", [WIDTH, HID1])
        dense_part = sb("dense_part", [P, M1, BATCH])
        wt1_sb = sb("wt1_sb", [P, 2, HID1])
        b1_sb = sb("b1_sb", [P, M1])
        wt2_sb = sb("wt2_sb", [P, M1, HID2])
        b2_sb = sb("b2_sb", [P, M2])
        wt3_sb = sb("wt3_sb", [P, M2])
        hid1_sum = sb("hid1_sum", [P, M1, P])
        hid1 = sb("hid1", [P, M1, P])
        hid2 = sb("hid2", [P, M2, P])
        y_sb = sb("y_sb", [1, BATCH])

        pick_ps = [pb("pick_ps0"), pb("pick_ps1")]
        x1_ps = [pb("x1_ps0"), pb("x1_ps1")]
        gram_ps = [pb("gram_ps0"), pb("gram_ps1")]
        spread_ps = pb("spread_ps")
        misc_ps = pb("misc_ps")

        ids_loaded = sem("ids_loaded")
        consts_loaded = sem("consts_loaded")
        dense_loaded = sem("dense_loaded")
        w0_loaded = sem("w0_loaded")
        w1_loaded = sem("w1_loaded")
        mlp_loaded = sem("mlp_loaded")
        constants_ready = sem("constants_ready")
        w0_ready = sem("w0_ready")
        dense_done = sem("dense_done")
        dense_copied = sem("dense_copied")
        rows_ready = sem("rows_ready")
        rows_seen = sem("rows_seen")
        gathered = sem("gathered")
        split_step = sem("split_step")
        split_done = sem("split_done")
        turned = sem("turned")
        cols_copied = sem("cols_copied")
        cols_copied_2 = sem("cols_copied_2")
        picked = sem("picked")
        left_copied = sem("left_copied")
        pairs_done = sem("pairs_done")
        spread_done = sem("spread_done")
        diag_done = sem("diag_done")
        x1_done = sem("x1_done")
        x1_copied = sem("x1_copied")
        gram_done = sem("gram_done")
        gram_copied = sem("gram_copied")
        z2_done = sem("z2_done")
        z2_copied = sem("z2_copied")
        hid1_done = sem("hid1_done")
        hid1_added = sem("hid1_added")
        hid1_ready = sem("hid1_ready")
        hid2_done = sem("hid2_done")
        hid2_ready = sem("hid2_ready")
        score_done = sem("score_done")
        score_copied = sem("score_copied")
        stored = sem("stored")

        block = ctx.enter_context(nc.Block())

        def turned_view(bank):
            return bank[0:PF, :].bitcast(BF16).rearrange("p (d b) -> p b d", b=P)

        @block.sync
        def _(sp):
            sp.dma_start(ids_sb[:], ids).then_inc(ids_loaded, 16)
            sp.dma_start(consts_sb[:], consts).then_inc(consts_loaded, 16)
            for dst, src in ((dense_sb[:], dense), (wtd_sb[:], wtd), (b1_sb[:], b1)):
                sp.dma_start(dst, src).then_inc(dense_loaded, 16)
            for dst, src in ((w0[0:PAIRS], w0a), (w0_other[0:PAIRS], w0b)):
                sp.dma_start(dst, src).then_inc(w0_loaded, 16)
            sp.dma_start(w1_sb[:], w1).then_inc(w1_loaded, 16)
            for dst, src in ((wt1_sb[:], wt1), (wt2_sb[:], wt2), (b2_sb[:], b2), (wt3_sb[:], wt3)):
                sp.dma_start(dst, src).then_inc(mlp_loaded, 16)
            sp.wait_ge(score_copied, TILES)
            sp.dma_start(out, y_sb[:]).then_inc(stored, 16)
            sp.wait_ge(stored, 16)

        @block.gpsimd
        def _(pool):
            def gather(k):
                nc.gpsimd.tensor_copy(rows_now[:], ids_sb[:, bass.ds(k, 1), :]).then_inc(rows_ready, 1)
                pool.wait_ge(rows_ready, k + 1)
                pool.sem_inc(rows_seen, 1)
                for f in range(FIELDS):
                    pool.indirect_dma_start(
                        out=emb[:, f, :], out_offset=None, in_=tables[f],
                        in_offset=bass.IndirectOffsetOnAxis(ap=rows_now[:, f:f + 1], axis=0),
                    ).then_inc(gathered, 16)

            pool.wait_ge(ids_loaded, 16)
            gather(0)
            with pool.Fori(1, TILES) as k:
                pool.wait_ge(split_done, k)
                gather(k)

        @block.scalar
        def _(act):
            def copy_dense():
                act.wait_ge(dense_loaded, 48)
                for n in range(2 * M1):
                    m, half = n // 2, n % 2
                    act.wait_ge(dense_done, n + 1)
                    nc.scalar.activation(dense_part[:, m, half * 512:half * 512 + 512], x1_ps[n % 2][:],
                                         ACT.Identity, bias=b1_sb[:, m:m + 1]).then_inc(dense_copied, 1)

            def copy_cols(k):
                act.wait_ge(turned, 2 * k + 1)
                nc.scalar.copy(cols[0:PF, :, 0:HALF], turned_view(spread_ps)).then_inc(cols_copied, 1)

            def copy_left(c, first=False):
                act.wait_ge(picked, ITEMS * c + 1)
                if not first:
                    act.wait_ge(pairs_done, GROUPS * c)
                nc.scalar.copy(left[0:PAIRS], pick_ps[0][0:PAIRS]).then_inc(left_copied, 1)

            def copy_x1(c, first=False):
                act.wait_ge(x1_done, c + 1)
                if not first:
                    act.wait_ge(gram_done, BLOCKS * c)
                return c

            def copy_x1_of(bank, c, first=False):
                copy_x1(c, first)
                nc.scalar.copy(x1_sb[:], x1_ps[bank][:].rearrange("p (q i) -> p q i", i=H)
                               ).then_inc(x1_copied, 1)

            def copy_gram(k, s, q):
                act.wait_ge(gram_done, BLOCKS * (CHUNKS * k + s) + q + 1)
                b = s * CB + q * BB
                nc.scalar.copy(gram[:, :, b:b + BB],
                               gram_ps[q % 2][:, 0:J * BB].rearrange("p (j b) -> p j b", b=BB)
                               ).then_inc(gram_copied, 1)

            def copy_z2(k):
                act.wait_ge(z2_done, k + 1)
                nc.scalar.copy(z2_sb[:], misc_ps[:, 0:P]).then_inc(z2_copied, 1)

            def relu_hid2(k, first=False):
                act.wait_ge(hid2_done, k + 1)
                if not first:
                    act.wait_ge(score_done, k)
                for m in range(M2):
                    nc.scalar.activation(hid2[:, m, :], misc_ps[:, m * P:(m + 1) * P], ACT.Relu,
                                         bias=b2_sb[:, m:m + 1]).then_inc(hid2_ready, 1)

            def copy_score(k):
                act.wait_ge(score_done, k + 1)
                nc.scalar.copy(y_sb[:, bass.ds(k * P, P)], misc_ps[0:1, 0:P]).then_inc(score_copied, 1)

            def tile(k, first=False, second=False, last=False):
                for s in range(CHUNKS):
                    c = CHUNKS * k + s
                    grams = not (first and s == 0)
                    gk, gs = (k - 1, CHUNKS - 1) if s == 0 else (k, s - 1)
                    if grams:
                        copy_x1_of(gs % 2, c - 1, first=first and s == 1)
                    if s == 1 and not first:
                        act.wait_ge(hid1_done, k)
                    if s < 3:
                        copy_left(c + 1)
                        for q in range(BLOCKS) if grams else ():
                            copy_gram(gk, gs, q)
                            if s == 2 and q == 2 and not first:
                                relu_hid2(k - 1, first=second)
                        if s == 0 and not first:
                            copy_z2(k - 1)
                    elif last:
                        for q in range(BLOCKS):
                            copy_gram(gk, gs, q)
                    else:
                        copy_cols(k + 1)
                        copy_gram(gk, gs, 0)
                        copy_left(c + 1)
                        copy_gram(gk, gs, 1)
                        copy_gram(gk, gs, 2)
                        copy_gram(gk, gs, 3)
                    if s == 3 and not first:
                        copy_score(k - 1)

            copy_dense()
            act.wait_ge(constants_ready, 3)
            copy_cols(0)
            copy_left(0, first=True)
            act.wait_ge(mlp_loaded, 64)
            tile(0, first=True)
            tile(1, second=True)
            with act.Fori(2, TILES - 1) as k:
                tile(k)
            tile(TILES - 1, last=True)
            end = TILES - 1
            copy_x1_of((CHUNKS - 1) % 2, CHUNKS * TILES - 1)
            for q in range(BLOCKS):
                copy_gram(end, CHUNKS - 1, q)
            copy_z2(end)
            relu_hid2(end)
            copy_score(end)

        @block.vector
        def _(dve):
            def split(k, first=False):
                dve.wait_ge(gathered, 16 * FIELDS * (k + 1))
                if not first:
                    dve.wait_ge(turned, 2 * k)
                nc.vector.tensor_copy(parts[:, 0], emb[:]).then_inc(split_step, 1)
                dve.wait_ge(split_step, 3 * k + 1)
                nc.vector.tensor_tensor(rest[:], emb[:], parts[:, 0], ALU.subtract).then_inc(split_step, 1)
                dve.wait_ge(split_step, 3 * k + 2)
                nc.vector.tensor_copy(parts[:, 1], rest[:]).then_inc(split_step, 1)
                dve.wait_ge(split_step, 3 * k + 3)
                nc.vector.tensor_tensor(parts[:, 2], rest[:], parts[:, 1], ALU.subtract).then_inc(split_done, 1)

            def copy_cols(k):
                dve.wait_ge(turned, 2 * k + 2)
                nc.vector.tensor_copy(cols[0:PF, :, HALF:WIDTH], turned_view(misc_ps)).then_inc(cols_copied_2, 1)

            def multiply(c, buf, g):
                dve.wait_ge(picked, ITEMS * c + g + 2)
                n = GROUP_ROWS[g]
                nc.vector.tensor_tensor(pairs[0:n, buf, g, :], pick_ps[(g + 1) % 2][0:n], left[0:n], ALU.mult
                                        ).then_inc(pairs_done, 1)

            def diagonal(c, buf, first=False):
                dve.wait_ge(spread_done, c + 1)
                if not first:
                    dve.wait_ge(gram_done, BLOCKS * (c - 1))
                e = spread_ps[:, 0:BLOCKS * J].rearrange("p (q j) -> p q j", j=J)
                nc.vector.tensor_tensor(
                    spread_e[:, buf], e[:, :, :, None].to_broadcast([P, BLOCKS, J, BB]),
                    consts_sb[:, None, None, C_MASK:C_ALL].to_broadcast([P, BLOCKS, J, BB]),
                    ALU.mult).then_inc(diag_done, 1)

            def hidden1(k, first=False):
                dve.wait_ge(hid1_done, k + 1)
                nc.vector.tensor_tensor(hid1_sum[:], misc_ps[:].rearrange("p (m b) -> p m b", b=P),
                                        dense_part[:, :, bass.ds(k * P, P)], ALU.add).then_inc(hid1_added, 1)
                dve.wait_ge(hid1_added, k + 1)
                if not first:
                    dve.wait_ge(hid2_done, k)
                nc.vector.tensor_scalar(hid1[:], hid1_sum[:], 0.0, None, ALU.max).then_inc(hid1_ready, 1)

            def chunk(c, buf, early=False, between=None):
                if not early:
                    dve.wait_ge(x1_done, c - 1)
                dve.wait_ge(left_copied, c + 1)
                for g in range(GROUPS):
                    multiply(c, buf, g)
                    if g == 0 and between is not None:
                        between()

            def tile(k, first=False, second=False, last=False):
                for s in range(CHUNKS):
                    if s == 3 and last:
                        break
                    if s == 3:
                        copy_cols(k + 1)
                    mlp = None
                    if s == 1 and not first:
                        def mlp():
                            hidden1(k - 1, first=second)
                    chunk(CHUNKS * k + s + 1, (s + 1) % 2, early=first and s == 0, between=mlp)
                    diagonal(CHUNKS * k + s + 1, (s + 1) % 2, first=first and s == 0)
                    if s == (2 if first or second else 1) and not last:
                        split(k + 1)

            dve.wait_ge(consts_loaded, 16)
            nc.vector.tensor_copy(consts_bf[:], consts_sb[:, 0:C_MASK]).then_inc(constants_ready, 1)
            nc.vector.memset(cols[96:P], 1.0).then_inc(constants_ready, 2)
            dve.wait_ge(w0_loaded, 32)
            nc.vector.tensor_tensor(w0[0:PAIRS], w0[0:PAIRS], w0_other[0:PAIRS], ALU.add).then_inc(w0_ready, 1)
            split(0, first=True)
            copy_cols(0)
            chunk(0, 0, early=True)
            diagonal(0, 0, first=True)
            tile(0, first=True)
            dve.wait_ge(dense_copied, 2 * M1)
            tile(1, second=True)
            with dve.Fori(2, TILES - 1) as k:
                tile(k)
            tile(TILES - 1, last=True)
            hidden1(TILES - 1)

        @block.tensor
        def _(pe):
            def dense_products():
                pe.wait_ge(dense_loaded, 48)
                for n in range(2 * M1):
                    m, half = n // 2, n % 2
                    if n >= 2:
                        pe.wait_ge(dense_copied, n - 1)
                    nc.tensor.matmul(x1_ps[n % 2][:], wtd_sb[:, m * P:(m + 1) * P],
                                     dense_sb[:, half * 512:half * 512 + 512],
                                     start=True, stop=True).then_inc(dense_done, 1)

            def turn(k, half, first=False, used=None):
                if half == 0:
                    pe.wait_ge(split_done, k + 1)
                    if not first:
                        pe.wait_ge(diag_done, CHUNKS * k)
                elif used is not None:
                    pe.wait_ge(hid2_ready, M2 * used)
                out_ps = (spread_ps, misc_ps)[half][0:PF, :].bitcast(BF16)
                for n in range(HALF):
                    mm = nc.tensor.transpose(out_ps[:, n * P:(n + 1) * P],
                                             parts[:, :, :, half * HALF + n].rearrange("p a f -> p (a f)"),
                                             consts_bf[:, C_IDENT:C_IDENT + P])
                mm.then_inc(turned, 1)

            def spread(s, c, first=False):
                if not first:
                    pe.wait_ge(diag_done, c)
                for q in range(BLOCKS):
                    b = s * CB + q * BB
                    mm = nc.tensor.matmul(spread_ps[:, q * J:(q + 1) * J], cols[0:PF + 1, b:b + BB, :].rearrange("p b d -> p (b d)"),
                                          consts_bf[0:PF + 1, C_SPREAD:C_SPREAD + J], start=True, stop=True)
                mm.then_inc(spread_done, 1)

            def pick(k, s, c, m, first=False):
                if m == 0 and s == 0:
                    pe.wait_ge(cols_copied, k + 1)
                    pe.wait_ge(cols_copied_2, k + 1)
                if m == 0 and not first:
                    pe.wait_ge(pairs_done, GROUPS * c - 1)
                if m == 1 and not first:
                    pe.wait_ge(pairs_done, GROUPS * c)
                if m == 2:
                    pe.wait_ge(left_copied, c + 1)
                if m >= 3:
                    pe.wait_ge(pairs_done, GROUPS * c + m - 2)
                n = PAIRS if m == 0 else GROUP_ROWS[m - 1]
                at = C_PICK + m * PAIRS
                nc.tensor.matmul(pick_ps[m % 2][0:n, :], consts_bf[0:PF, at:at + n],
                                 cols[0:PF, s * CB:(s + 1) * CB, :], start=True, stop=True).then_inc(picked, 1)

            def sum_pairs(c, buf, g, early=False):
                if g == 0:
                    pe.wait_ge(pairs_done, GROUPS * c + 2)
                    if not early:
                        pe.wait_ge(x1_copied, c - 1)
                if g == 2:
                    pe.wait_ge(pairs_done, GROUPS * c + 4)
                if g == 4:
                    pe.wait_ge(pairs_done, GROUPS * c + 7)
                n = GROUP_ROWS[g]
                for q in range(BLOCKS):
                    mm = nc.tensor.matmul(x1_ps[buf][:, q * H:(q + 1) * H],
                                          pairs[0:n, buf, g, q * P:(q + 1) * P], w0[0:n, g, :],
                                          start=(g == 0 and q == 0), stop=(g == GROUPS - 1),
                                          skip_group_check=True)
                if g == GROUPS - 1:
                    mm.then_inc(x1_done, 1)

            def gram_block(c, buf, q, early=False):
                if q == 0:
                    pe.wait_ge(x1_copied, c + 1)
                    pe.wait_ge(diag_done, c + 1)
                if not (early and q < 2):
                    pe.wait_ge(gram_copied, BLOCKS * c + q - 1)
                nc.tensor.matmul(gram_ps[q % 2][:, 0:J * BB], x1_sb[:, q, :],
                                 spread_e[:, buf, q].rearrange("p j b -> p (j b)"),
                                 start=True, stop=True).then_inc(gram_done, 1)

            def second_layer(k, first=False):
                if not first:
                    pe.wait_ge(score_copied, k)
                pe.wait_ge(gram_copied, CHUNKS * BLOCKS * (k + 1))
                for j in range(FIELDS):
                    mm = nc.tensor.matmul(misc_ps[:, 0:P], w1_sb[:, j, :], gram[:, j, :],
                                          start=(j == 0), stop=(j == FIELDS - 1))
                mm.then_inc(z2_done, 1)

            def mlp1(k):
                pe.wait_ge(z2_copied, k + 1)
                for m in range(M1):
                    at = misc_ps[:, m * P:(m + 1) * P]
                    nc.tensor.matmul(at, wt1_sb[:, 0, m * P:(m + 1) * P], gram[:, FIELDS, :], start=True, stop=False)
                    mm = nc.tensor.matmul(at, wt1_sb[:, 1, m * P:(m + 1) * P], z2_sb[:], start=False, stop=True)
                mm.then_inc(hid1_done, 1)

            def mlp2(k):
                pe.wait_ge(hid1_ready, k + 1)
                for m in range(M2):
                    for n in range(M1):
                        mm = nc.tensor.matmul(misc_ps[:, m * P:(m + 1) * P], wt2_sb[:, n, m * P:(m + 1) * P],
                                              hid1[:, n, :], start=(n == 0), stop=(n == M1 - 1))
                mm.then_inc(hid2_done, 1)

            def mlp3(k):
                pe.wait_ge(hid2_ready, M2 * (k + 1))
                for n in range(M2):
                    mm = nc.tensor.matmul(misc_ps[0:1, 0:P], wt3_sb[:, n:n + 1], hid2[:, n, :],
                                          start=(n == 0), stop=(n == M2 - 1))
                mm.then_inc(score_done, 1)

            early_picks = {0: (0, 1), 1: (2,), 2: (3, 4), 3: (5, 6), 4: (7,)}
            late_picks = {2: (0, 1), 3: (2,), 4: (3, 4), 5: (5, 6), 6: (7,)}
            picks = [early_picks] * (CHUNKS - 1) + [late_picks]

            def tile(k, first=False, second=False, last=False):
                for s in range(CHUNKS):
                    c = CHUNKS * k + s
                    buf, nbuf = s % 2, (s + 1) % 2
                    nk, ns = (k + 1, 0) if s == CHUNKS - 1 else (k, s + 1)
                    grams = not (first and s == 0)
                    prepare = not (last and s == CHUNKS - 1)
                    for g in range(GROUPS):
                        sum_pairs(c, buf, g, early=first and s < 2)
                        if s == CHUNKS - 1 and prepare and g < 2:
                            turn(nk, g, used=None if first else k)
                        if grams and 1 <= g <= BLOCKS:
                            gram_block(c - 1, nbuf, g - 1, early=first and s == 1)
                        if prepare and g in picks[s]:
                            for m in picks[s][g]:
                                pick(nk, ns, c + 1, m)
                        if prepare and g == 3:
                            spread(ns, c + 1)
                        if not first:
                            if s == 1 and g == 0:
                                mlp1(k - 1)
                            if s == 2 and g == 2:
                                mlp2(k - 1)
                            if s == 3 and g == 4:
                                mlp3(k - 1)
                    if not first and s == 0:
                        second_layer(k - 1, first=second)

            dense_products()
            pe.wait_ge(constants_ready, 3)
            pe.wait_ge(dense_copied, 2 * M1)
            turn(0, 0, first=True)
            turn(0, 1)
            for m in range(ITEMS):
                pick(0, 0, 0, m, first=True)
            spread(0, 0, first=True)
            pe.wait_ge(w0_ready, 1)
            tile(0, first=True)
            pe.wait_ge(w1_loaded, 16)
            pe.wait_ge(mlp_loaded, 64)
            tile(1, second=True)
            with pe.Fori(2, TILES - 1) as k:
                tile(k)
            tile(TILES - 1, last=True)
            end = TILES - 1
            for q in range(BLOCKS):
                gram_block(CHUNKS * TILES - 1, (CHUNKS - 1) % 2, q)
            second_layer(end)
            mlp1(end)
            mlp2(end)
            mlp3(end)


def constants():
    import numpy as np

    c = np.zeros((P, C_ALL), np.float32)
    for part in range(PARTS):
        for r in range(R):
            for k in range(FIELDS):
                c[part * FIELDS + (k - r) % FIELDS, C_PICK + r * FIELDS + k] = 1
                for g in range(GROUPS):
                    c[part * FIELDS + (k + R * g) % FIELDS, C_PICK + (g + 1) * PAIRS + r * FIELDS + k] = 1
        for j in range(FIELDS):
            c[part * FIELDS + j, C_SPREAD + j] = 1
    c[PF, C_SPREAD + FIELDS] = 1
    c[:, C_IDENT:C_IDENT + P] = np.eye(P)
    for p in range(P):
        c[p, C_MASK + p // WIDTH] = 1
    return c


def pair_fields():
    import numpy as np

    r = np.arange(PAIRS) // FIELDS
    k = np.arange(PAIRS) % FIELDS
    g = np.arange(GROUPS)[:, None]
    return np.broadcast_to((k - r) % FIELDS, (GROUPS, PAIRS)), (k + R * g) % FIELDS


def kernel(**inputs):
    import numpy as np
    import concourse.bacc as bacc
    from concourse.bass_utils import run_bass_kernel_spmd

    x = {n: np.asarray(a) for n, a in inputs.items()}
    lf, rt = pair_fields()
    used = np.arange(PAIRS)[None, :] < np.array(GROUP_ROWS)[:, None]
    w = x["L0_rec_W0"].reshape(H, FIELDS, FIELDS)
    w0a = np.where(used[:, :, None], w[:, lf, rt].transpose(1, 2, 0), np.float32(0)).transpose(1, 0, 2)
    w0b = np.where((used & (lf != rt))[:, :, None], w[:, rt, lf].transpose(1, 2, 0), np.float32(0)).transpose(1, 0, 2)
    arrays = {
        "ids": x["ids"].reshape(TILES, P, FIELDS).transpose(1, 0, 2),
        **{f"tbl_{f}": x[f"tbl_{f}"] for f in range(FIELDS)},
        "consts": constants(),
        "w0a": w0a,
        "w0b": w0b,
        "w1": x["L0_rec_W1"].reshape(H, H, FIELDS).transpose(1, 2, 0),
        "dense": x["dense_ctx"].T,
        "wt1": x["W_top1"][0:2 * H].reshape(2, H, HID1).transpose(1, 0, 2),
        "wtd": x["W_top1"][2 * H:],
        "b1": x["b_top1"].reshape(M1, P).T,
        "wt2": x["W_top2"].reshape(M1, P, HID2).transpose(1, 0, 2),
        "b2": x["b_top2"].reshape(M2, P).T,
        "wt3": x["W_top3"].reshape(M2, P).T,
    }
    nc = bacc.Bacc("TRN2", target_bir_lowering=False, num_devices=1)
    aps = {}
    for name, a in arrays.items():
        arrays[name] = np.ascontiguousarray(a)
        aps[name] = nc.dram_tensor(f"{name}_dram", a.shape, mybir.dt.from_np(a.dtype), kind="ExternalInput").ap()
    out = nc.dram_tensor("y_dram", (1, BATCH), F32, kind="ExternalOutput").ap()
    build(nc, aps["ids"], [aps[f"tbl_{f}"] for f in range(FIELDS)],
          *[aps[n] for n in ("consts", "w0a", "w0b", "w1", "dense", "wt1", "wtd", "b1", "wt2", "b2", "wt3")], out)
    r = run_bass_kernel_spmd(nc, [{f"{n}_dram": a for n, a in arrays.items()}], core_ids=[0])
    return r.results[0]["y_dram"].reshape(BATCH, 1)
```

```python
from contextlib import ExitStack

import concourse.bass as bass
from concourse import mybir

F32 = mybir.dt.float32
BF16 = mybir.dt.bfloat16
I32 = mybir.dt.int32
ALU = mybir.AluOpType
ACT = mybir.ActivationFunctionType

P = 128
FIELDS = 39
WIDTH = 16
BATCH = 1024
TILES = BATCH // P
CHUNKS = 4
CB = P // CHUNKS
COLS = WIDTH * CB
BLOCKS = 4
BB = CB // BLOCKS
PARTS = 3
R = 3
GROUPS = 7
PAIRS = R * FIELDS
GROUP_ROWS = [PAIRS] * 6 + [2 * FIELDS]
LEFTS, RIGHTS = 2, 4
ITEMS = LEFTS + RIGHTS
SUM_ORDER = [(0, 0), (0, 4), (1, 1), (1, 5), (2, 2), (2, 6), (3, 3)]
PF = PARTS * FIELDS
J = FIELDS + 1
H = 128
HID1, HID2 = 512, 256
M1, M2 = HID1 // P, HID2 // P
HALF = WIDTH // 2
SMALL = 16
SP = 125
DEPTHS = (8, 10)
BATCHES = ((0, 4), (4, 10), (10, 16))
HOTS = 4
HALF_SMALL = SMALL // 2

C_PICK = 0
C_SPREAD = C_PICK + ITEMS * PAIRS
C_IDENT = C_SPREAD + J
C_MASK = C_IDENT + P
C_ROWS = C_MASK + BB
C_ALL = C_ROWS + sum(DEPTHS)


def build(nc, ids, ids_small, tables, consts, w0a, w0b, w1, dense, wt1, wtd, b1, wt2, b2, wt3, out):
    depth = [t.shape[0] // SP for t in tables[0:SMALL]]
    first_slot = [sum(depth[0:f]) for f in range(SMALL + 1)]
    slots = first_slot[SMALL]
    rows_at = [sum(DEPTHS[0:DEPTHS.index(d)]) for d in depth]

    with ExitStack() as ctx:
        def sb(name, shape, dt=F32):
            return ctx.enter_context(nc.sbuf_tensor(name, shape, dt))

        def pb(name):
            return ctx.enter_context(nc.psum_tensor(name, [P, 512], F32))

        def sem(name):
            return ctx.enter_context(nc.semaphore(name))

        ids_sb = sb("ids_sb", [P, TILES, FIELDS], I32)
        rows_now = sb("rows_now", [P, 2, FIELDS], I32)
        consts_sb = sb("consts_sb", [P, C_ALL])
        consts_bf = sb("consts_bf", [P, C_MASK], BF16)
        emb = sb("emb", [P, 2, FIELDS, WIDTH])
        rest = sb("rest", [P, FIELDS, WIDTH])
        parts = sb("parts", [P, PARTS, FIELDS, WIDTH], BF16)
        cols = sb("cols", [P, P, WIDTH], BF16)
        left = sb("left", [P, LEFTS, COLS])
        pairs = sb("pairs", [P, 2, GROUPS, COLS])
        w0 = sb("w0", [P, GROUPS, H])
        w0_other = sb("w0_other", [P, GROUPS, H])
        w1_sb = sb("w1_sb", [P, FIELDS, H])
        spread_e = sb("spread_e", [P, 2, BLOCKS, J, BB])
        x1_sb = sb("x1_sb", [P, BLOCKS, H])
        gram = sb("gram", [P, J, P])
        z2_sb = sb("z2_sb", [P, P])
        dense_sb = sb("dense_sb", [WIDTH, BATCH])
        wtd_sb = sb("wtd_sb", [WIDTH, HID1])
        dense_part = sb("dense_part", [P, M1, BATCH])
        wt1_sb = sb("wt1_sb", [P, 2, HID1])
        b1_sb = sb("b1_sb", [P, M1])
        wt2_sb = sb("wt2_sb", [P, M1, HID2])
        b2_sb = sb("b2_sb", [P, M2])
        wt3_sb = sb("wt3_sb", [P, M2])
        hid1_sum = sb("hid1_sum", [P, M1, P])
        hid1 = sb("hid1", [P, M1, P])
        hid2 = sb("hid2", [P, M2, P])
        y_sb = sb("y_sb", [1, BATCH])

        F16 = mybir.dt.float16
        gram_flat = gram[:].rearrange("p j b -> p (j b)")
        small_tab = gram_flat[:, 0:slots * WIDTH].rearrange("p (m d) -> p m d", d=WIDTH)
        small_rest = gram_flat[:, slots * WIDTH:2 * slots * WIDTH].rearrange("p (m d) -> p m d", d=WIDTH)
        pairs_flat = pairs[:].rearrange("p u g n -> p (u g n)")
        small_words = slots * PARTS * WIDTH // 2
        small_parts = pairs_flat[:, 0:small_words].bitcast(BF16).rearrange("p (m a d) -> p m a d", a=PARTS, d=WIDTH)
        ids_words = SMALL * P // 2
        ids_f16 = pairs_flat[:, small_words:small_words + ids_words].bitcast(F16).rearrange("p (f b) -> p f b", b=P)
        ids_rep = pairs_flat[:, small_words + ids_words:small_words + 3 * ids_words].bitcast(I32)
        spread_flat = spread_e[:].rearrange("p u q j b -> p (u q j b)")
        rows_words = sum(DEPTHS) * P // 2
        row_numbers = spread_flat[:, 0:rows_words].bitcast(F16).rearrange("p (m b) -> p m b", b=P)
        hot = sb("hot", [P, HOTS, max(DEPTHS), P], BF16)

        pick_ps = [pb("pick_ps0"), pb("pick_ps1")]
        x1_ps = [pb("x1_ps0"), pb("x1_ps1")]
        gram_ps = [pb("gram_ps0"), pb("gram_ps1")]
        spread_ps = pb("spread_ps")
        misc_ps = pb("misc_ps")

        ids_loaded = sem("ids_loaded")
        consts_loaded = sem("consts_loaded")
        ids_rep_loaded = sem("ids_rep_loaded")
        small_loaded = [sem(f"small_loaded{n}") for n in range(len(BATCHES))]
        small_step = sem("small_step")
        small_rested = sem("small_rested")
        hot_done = sem("hot_done")
        hot_used = sem("hot_used")
        small_copied = sem("small_copied")
        dense_loaded = sem("dense_loaded")
        w0_loaded = sem("w0_loaded")
        w1_loaded = sem("w1_loaded")
        mlp_loaded = sem("mlp_loaded")
        constants_ready = sem("constants_ready")
        w0_ready = sem("w0_ready")
        dense_done = sem("dense_done")
        dense_copied = sem("dense_copied")
        rows_ready = sem("rows_ready")
        rows_seen = sem("rows_seen")
        gathered = [sem("gathered0"), sem("gathered1")]
        emb_read = sem("emb_read")
        split_step = sem("split_step")
        split_done = sem("split_done")
        turned = sem("turned")
        cols_copied = sem("cols_copied")
        cols_copied_2 = sem("cols_copied_2")
        picked = sem("picked")
        left_copied = sem("left_copied")
        pairs_done = sem("pairs_done")
        spread_done = sem("spread_done")
        diag_done = sem("diag_done")
        x1_done = sem("x1_done")
        x1_copied = sem("x1_copied")
        gram_done = sem("gram_done")
        gram_copied = sem("gram_copied")
        z2_done = sem("z2_done")
        z2_copied = sem("z2_copied")
        hid1_done = sem("hid1_done")
        hid1_added = sem("hid1_added")
        hid1_ready = sem("hid1_ready")
        hid2_done = sem("hid2_done")
        hid2_ready = sem("hid2_ready")
        score_done = sem("score_done")
        score_copied = sem("score_copied")
        stored = sem("stored")

        block = ctx.enter_context(nc.Block())

        def turned_view(bank):
            return bank[0:PF, :].bitcast(BF16).rearrange("p (d b) -> p b d", b=P)

        @block.sync
        def _(sp):
            sp.dma_start(ids_sb[:], ids).then_inc(ids_loaded, 16)
            sp.dma_start(ids_rep, ids_small.to_broadcast([P, SMALL * P])).then_inc(ids_rep_loaded, 16)
            sp.dma_start(consts_sb[:], consts).then_inc(consts_loaded, 16)
            for n, (lo, hi) in enumerate(BATCHES):
                for f in range(lo, hi):
                    sp.dma_start(small_tab[0:SP, first_slot[f]:first_slot[f + 1], :],
                                 tables[f].rearrange("(p m) d -> p m d", p=SP)).then_inc(small_loaded[n], 16)
                if n == 0:
                    for dst, src in ((dense_sb[:], dense), (wtd_sb[:], wtd), (b1_sb[:], b1)):
                        sp.dma_start(dst, src).then_inc(dense_loaded, 16)
            for dst, src in ((w0[0:PAIRS], w0a), (w0_other[0:PAIRS], w0b)):
                sp.dma_start(dst, src).then_inc(w0_loaded, 16)
            sp.dma_start(w1_sb[:], w1).then_inc(w1_loaded, 16)
            for dst, src in ((wt1_sb[:], wt1), (wt2_sb[:], wt2), (b2_sb[:], b2), (wt3_sb[:], wt3)):
                sp.dma_start(dst, src).then_inc(mlp_loaded, 16)
            sp.wait_ge(score_copied, TILES)
            sp.dma_start(out, y_sb[:]).then_inc(stored, 16)
            sp.wait_ge(stored, 16)

        @block.gpsimd
        def _(pool):
            def gather(k, parity, fields=range(FIELDS)):
                nc.gpsimd.tensor_copy(rows_now[:, parity:parity + 1, :], ids_sb[:, bass.ds(k, 1), :]
                                      ).then_inc(rows_ready, 1)
                pool.wait_ge(rows_ready, k + 1)
                pool.sem_inc(rows_seen, 1)
                for f in fields:
                    pool.indirect_dma_start(
                        out=emb[:, parity, f, :], out_offset=None, in_=tables[f],
                        in_offset=bass.IndirectOffsetOnAxis(ap=rows_now[:, parity, f:f + 1], axis=0),
                    ).then_inc(gathered[parity], 16)

            pool.wait_ge(ids_loaded, 16)
            gather(0, 0, range(SMALL, FIELDS))
            gather(1, 1)
            with pool.Fori(1, TILES // 2) as pair:
                k = 2 * pair
                pool.wait_ge(emb_read, k - 1)
                gather(k, 0)
                pool.wait_ge(emb_read, k)
                gather(k + 1, 1)

        @block.scalar
        def _(act):
            def small_batch_part(n, a):
                lo, hi = (first_slot[f] for f in BATCHES[n])
                if a == 0:
                    act.wait_ge(small_loaded[n], 16 * (BATCHES[n][1] - BATCHES[n][0]))
                else:
                    act.wait_ge(small_rested, 2 * n + 1)
                src = (small_tab, small_rest)[a]
                nc.scalar.copy(small_parts[0:SP, lo:hi, a, :], src[0:SP, lo:hi, :]).then_inc(small_step, 1)

            def copy_small(bank):
                act.wait_ge(hot_used, HALF_SMALL * (bank + 1))
                f = HALF_SMALL * bank
                nc.scalar.copy(parts[:, :, f:f + HALF_SMALL, :],
                               gram_ps[bank][:, 0:HALF_SMALL * PARTS * WIDTH].rearrange(
                                   "p (f a d) -> p a f d", a=PARTS, d=WIDTH)).then_inc(small_copied, 1)

            def copy_dense(steps):
                act.wait_ge(dense_loaded, 48)
                for n in steps:
                    m, half = n // 2, n % 2
                    act.wait_ge(dense_done, n + 1)
                    nc.scalar.activation(dense_part[:, m, half * 512:half * 512 + 512], x1_ps[n % 2][:],
                                         ACT.Identity, bias=b1_sb[:, m:m + 1]).then_inc(dense_copied, 1)

            def copy_cols(k):
                act.wait_ge(turned, 2 * k + 1)
                nc.scalar.copy(cols[0:PF, :, 0:HALF], turned_view(spread_ps)).then_inc(cols_copied, 1)

            def copy_left(c, first=False):
                for a in range(LEFTS):
                    act.wait_ge(picked, ITEMS * c + a + 1)
                    if a == 0 and not first:
                        act.wait_ge(pairs_done, RIGHTS * c)
                    nc.scalar.copy(left[0:PAIRS, a, :], pick_ps[a][0:PAIRS]).then_inc(left_copied, 1)

            def copy_x1(c, first=False):
                act.wait_ge(x1_done, c + 1)
                if not first:
                    act.wait_ge(gram_done, BLOCKS * c)
                return c

            def copy_x1_of(bank, c, first=False):
                copy_x1(c, first)
                nc.scalar.copy(x1_sb[:], x1_ps[bank][:].rearrange("p (q i) -> p q i", i=H)
                               ).then_inc(x1_copied, 1)

            def copy_gram(k, s, q):
                act.wait_ge(gram_done, BLOCKS * (CHUNKS * k + s) + q + 1)
                b = s * CB + q * BB
                nc.scalar.copy(gram[:, :, b:b + BB],
                               gram_ps[q % 2][:, 0:J * BB].rearrange("p (j b) -> p j b", b=BB)
                               ).then_inc(gram_copied, 1)

            def copy_z2(k):
                act.wait_ge(z2_done, k + 1)
                nc.scalar.copy(z2_sb[:], misc_ps[:, 0:P]).then_inc(z2_copied, 1)

            def relu_hid2(k, first=False):
                act.wait_ge(hid2_done, k + 1)
                if not first:
                    act.wait_ge(score_done, k)
                for m in range(M2):
                    nc.scalar.activation(hid2[:, m, :], misc_ps[:, m * P:(m + 1) * P], ACT.Relu,
                                         bias=b2_sb[:, m:m + 1]).then_inc(hid2_ready, 1)

            def copy_score(k):
                act.wait_ge(score_done, k + 1)
                nc.scalar.copy(y_sb[:, bass.ds(k * P, P)], misc_ps[0:1, 0:P]).then_inc(score_copied, 1)

            def tile(k, first=False, second=False, last=False):
                for s in range(CHUNKS):
                    c = CHUNKS * k + s
                    grams = not (first and s == 0)
                    gk, gs = (k - 1, CHUNKS - 1) if s == 0 else (k, s - 1)
                    if grams:
                        copy_x1_of(gs % 2, c - 1, first=first and s == 1)
                    if s == 1 and not first:
                        act.wait_ge(hid1_done, k)
                    if s < 3:
                        copy_left(c + 1)
                        for q in range(BLOCKS) if grams else ():
                            copy_gram(gk, gs, q)
                            if s == 2 and q == 2 and not first:
                                relu_hid2(k - 1, first=second)
                        if s == 0 and not first:
                            copy_z2(k - 1)
                    elif last:
                        for q in range(BLOCKS):
                            copy_gram(gk, gs, q)
                    else:
                        copy_cols(k + 1)
                        copy_gram(gk, gs, 0)
                        copy_left(c + 1)
                        copy_gram(gk, gs, 1)
                        copy_gram(gk, gs, 2)
                        copy_gram(gk, gs, 3)
                    if s == 3 and not first:
                        copy_score(k - 1)

            act.wait_ge(ids_rep_loaded, 16)
            nc.scalar.copy(ids_f16, ids_rep.rearrange("p (f b) -> p f b", b=P)).then_inc(small_step, 1)
            act.wait_ge(consts_loaded, 16)
            nc.scalar.copy(row_numbers, consts_sb[:, C_ROWS:C_ALL, None].to_broadcast([P, sum(DEPTHS), P])
                           ).then_inc(small_step, 1)
            small_batch_part(0, 0)
            small_batch_part(0, 1)
            copy_dense(range(0, 2))
            small_batch_part(1, 0)
            copy_dense(range(2, 4))
            small_batch_part(1, 1)
            small_batch_part(2, 0)
            copy_dense(range(4, 6))
            small_batch_part(2, 1)
            copy_dense(range(6, 8))
            copy_small(0)
            copy_small(1)
            act.wait_ge(constants_ready, 3)
            copy_cols(0)
            copy_left(0, first=True)
            act.wait_ge(mlp_loaded, 64)
            tile(0, first=True)
            tile(1, second=True)
            with act.Fori(2, TILES - 1) as k:
                tile(k)
            tile(TILES - 1, last=True)
            end = TILES - 1
            copy_x1_of((CHUNKS - 1) % 2, CHUNKS * TILES - 1)
            for q in range(BLOCKS):
                copy_gram(end, CHUNKS - 1, q)
            copy_z2(end)
            relu_hid2(end)
            copy_score(end)

        @block.vector
        def _(dve):
            def split(k, parity, first=False):
                at = SMALL if first else 0
                e, rest_e = emb[:, parity, at:, :], rest[:, at:, :]
                part = [parts[:, a, at:, :] for a in range(PARTS)]
                dve.wait_ge(gathered[parity], 8 * FIELDS * (k + 2 - parity) - (16 * SMALL if parity == 0 else 0))
                if not first:
                    dve.wait_ge(turned, 2 * k)
                nc.vector.tensor_copy(part[0], e).then_inc(split_step, 1)
                dve.wait_ge(split_step, 2 * k + 1)
                nc.vector.tensor_tensor(rest_e, e, part[0], ALU.subtract).then_inc(emb_read, 1)
                dve.wait_ge(emb_read, k + 1)
                nc.vector.tensor_copy(part[1], rest_e).then_inc(split_step, 1)
                dve.wait_ge(split_step, 2 * k + 2)
                nc.vector.tensor_tensor(part[2], rest_e, part[1], ALU.subtract).then_inc(split_done, 1)

            def small_rests(n, step):
                lo, hi = (first_slot[f] for f in BATCHES[n])
                rest_n, tab_n = small_rest[0:SP, lo:hi, :], small_tab[0:SP, lo:hi, :]
                part = [small_parts[0:SP, lo:hi, a, :] for a in range(PARTS)]
                dve.wait_ge(small_step, 2 + 2 * n + step + 1)
                if step == 0:
                    dve.wait_ge(small_loaded[n], 16 * (BATCHES[n][1] - BATCHES[n][0]))
                    nc.vector.tensor_tensor(rest_n, tab_n, part[0], ALU.subtract).then_inc(small_rested, 1)
                else:
                    nc.vector.tensor_tensor(part[2], rest_n, part[1], ALU.subtract).then_inc(small_rested, 1)

            def one_hot(f):
                if f >= HOTS:
                    dve.wait_ge(hot_used, f - HOTS + 1)
                nc.vector.tensor_tensor(hot[0:SP, f % HOTS, 0:depth[f], :],
                                        ids_f16[0:SP, f:f + 1, :].to_broadcast([SP, depth[f], P]),
                                        row_numbers[0:SP, rows_at[f]:rows_at[f] + depth[f], :],
                                        ALU.is_equal).then_inc(hot_done, 1)

            def copy_cols(k):
                dve.wait_ge(turned, 2 * k + 2)
                nc.vector.tensor_copy(cols[0:PF, :, HALF:WIDTH], turned_view(misc_ps)).then_inc(cols_copied_2, 1)

            def multiply(c, buf, b):
                dve.wait_ge(picked, ITEMS * c + LEFTS + b + 1)
                n = len(range(b, GROUPS, RIGHTS))
                nc.vector.tensor_tensor(pairs[0:PAIRS, buf, b:GROUPS:RIGHTS, :],
                                        pick_ps[b % 2][0:PAIRS, None, :].to_broadcast([PAIRS, n, COLS]),
                                        left[0:PAIRS, 0:n, :], ALU.mult).then_inc(pairs_done, 1)

            def diagonal(c, buf, first=False):
                dve.wait_ge(spread_done, c + 1)
                if not first:
                    dve.wait_ge(gram_done, BLOCKS * (c - 1))
                e = spread_ps[:, 0:BLOCKS * J].rearrange("p (q j) -> p q j", j=J)
                nc.vector.tensor_tensor(
                    spread_e[:, buf], e[:, :, :, None].to_broadcast([P, BLOCKS, J, BB]),
                    consts_sb[:, None, None, C_MASK:C_ROWS].to_broadcast([P, BLOCKS, J, BB]),
                    ALU.mult).then_inc(diag_done, 1)

            def hidden1(k, first=False):
                dve.wait_ge(hid1_done, k + 1)
                nc.vector.tensor_tensor(hid1_sum[:], misc_ps[:].rearrange("p (m b) -> p m b", b=P),
                                        dense_part[:, :, bass.ds(k * P, P)], ALU.add).then_inc(hid1_added, 1)
                dve.wait_ge(hid1_added, k + 1)
                if not first:
                    dve.wait_ge(hid2_done, k)
                nc.vector.tensor_scalar(hid1[:], hid1_sum[:], 0.0, None, ALU.max).then_inc(hid1_ready, 1)

            def chunk(c, buf, early=False, between=None):
                if not early:
                    dve.wait_ge(x1_done, c - 1)
                dve.wait_ge(left_copied, LEFTS * (c + 1))
                for b in range(RIGHTS):
                    multiply(c, buf, b)
                    if b == 0 and between is not None:
                        between()

            def tile(k, parity, first=False, second=False, last=False):
                for s in range(CHUNKS):
                    if s == 3 and last:
                        break
                    if s == 3:
                        copy_cols(k + 1)
                    mlp = None
                    if s == 1 and not first:
                        def mlp():
                            hidden1(k - 1, first=second)
                    chunk(CHUNKS * k + s + 1, (s + 1) % 2, early=first and s == 0, between=mlp)
                    diagonal(CHUNKS * k + s + 1, (s + 1) % 2, first=first and s == 0)
                    if s == (2 if first or second else 1) and not last:
                        split(k + 1, 1 - parity)

            dve.wait_ge(consts_loaded, 16)
            nc.vector.tensor_copy(consts_bf[:], consts_sb[:, 0:C_MASK]).then_inc(constants_ready, 1)
            nc.vector.memset(cols[96:P], 1.0).then_inc(constants_ready, 2)
            for n, (lo, hi) in enumerate(BATCHES):
                small_rests(n, 0)
                for f in range(lo, lo + 2):
                    one_hot(f)
                small_rests(n, 1)
                for f in range(lo + 2, hi):
                    one_hot(f)
            dve.wait_ge(w0_loaded, 32)
            nc.vector.tensor_tensor(w0[0:PAIRS], w0[0:PAIRS], w0_other[0:PAIRS], ALU.add).then_inc(w0_ready, 1)
            split(0, 0, first=True)
            dve.wait_ge(small_copied, 2)
            copy_cols(0)
            chunk(0, 0, early=True)
            diagonal(0, 0, first=True)
            tile(0, 0, first=True)
            dve.wait_ge(dense_copied, 2 * M1)
            tile(1, 1, second=True)
            with dve.Fori(1, TILES // 2 - 1) as pair:
                k = 2 * pair
                tile(k, 0)
                tile(k + 1, 1)
            tile(TILES - 2, 0)
            tile(TILES - 1, 1, last=True)
            hidden1(TILES - 1)

        @block.tensor
        def _(pe):
            def small_field(f):
                batch = next(n for n, (lo, hi) in enumerate(BATCHES) if lo <= f < hi)
                if f == BATCHES[batch][0]:
                    pe.wait_ge(small_rested, 2 * batch + 2)
                pe.wait_ge(hot_done, f + 1)
                at = f % HALF_SMALL * PARTS * WIDTH
                for m in range(depth[f]):
                    mm = nc.tensor.matmul(gram_ps[f // HALF_SMALL][:, at:at + PARTS * WIDTH],
                                          hot[0:SP, f % HOTS, m, :],
                                          small_parts[0:SP, first_slot[f] + m, :, :].rearrange("p a d -> p (a d)"),
                                          start=(m == 0), stop=(m == depth[f] - 1))
                mm.then_inc(hot_used, 1)

            def dense_products(steps):
                pe.wait_ge(dense_loaded, 48)
                for n in steps:
                    m, half = n // 2, n % 2
                    if n >= 2:
                        pe.wait_ge(dense_copied, n - 1)
                    nc.tensor.matmul(x1_ps[n % 2][:], wtd_sb[:, m * P:(m + 1) * P],
                                     dense_sb[:, half * 512:half * 512 + 512],
                                     start=True, stop=True).then_inc(dense_done, 1)

            def turn(k, half, first=False, used=None):
                if half == 0:
                    pe.wait_ge(split_done, k + 1)
                    if not first:
                        pe.wait_ge(diag_done, CHUNKS * k)
                elif used is not None:
                    pe.wait_ge(hid2_ready, M2 * used)
                out_ps = (spread_ps, misc_ps)[half][0:PF, :].bitcast(BF16)
                for n in range(HALF):
                    mm = nc.tensor.transpose(out_ps[:, n * P:(n + 1) * P],
                                             parts[:, :, :, half * HALF + n].rearrange("p a f -> p (a f)"),
                                             consts_bf[:, C_IDENT:C_IDENT + P])
                mm.then_inc(turned, 1)

            def spread(s, c, first=False):
                if not first:
                    pe.wait_ge(diag_done, c)
                for q in range(BLOCKS):
                    b = s * CB + q * BB
                    mm = nc.tensor.matmul(spread_ps[:, q * J:(q + 1) * J], cols[0:PF + 1, b:b + BB, :].rearrange("p b d -> p (b d)"),
                                          consts_bf[0:PF + 1, C_SPREAD:C_SPREAD + J], start=True, stop=True)
                mm.then_inc(spread_done, 1)

            def pick(k, s, c, m, first=False):
                if m == 0 and s == 0:
                    pe.wait_ge(cols_copied, k + 1)
                    pe.wait_ge(cols_copied_2, k + 1)
                if m < LEFTS:
                    if not first:
                        pe.wait_ge(pairs_done, RIGHTS * c + m - 1)
                elif m < 2 * LEFTS:
                    pe.wait_ge(left_copied, LEFTS * c + m - 1)
                else:
                    pe.wait_ge(pairs_done, RIGHTS * c + m - 3)
                at = C_PICK + m * PAIRS
                nc.tensor.matmul(pick_ps[m % 2][0:PAIRS, :], consts_bf[0:PF, at:at + PAIRS],
                                 cols[0:PF, s * CB:(s + 1) * CB, :], start=True, stop=True).then_inc(picked, 1)

            def sum_pairs(c, buf, step, early=False):
                b, g = SUM_ORDER[step]
                if g < RIGHTS:
                    pe.wait_ge(pairs_done, RIGHTS * c + b + 1)
                if step == 0 and not early:
                    pe.wait_ge(x1_copied, c - 1)
                n = GROUP_ROWS[g]
                for q in range(BLOCKS):
                    mm = nc.tensor.matmul(x1_ps[buf][:, q * H:(q + 1) * H],
                                          pairs[0:n, buf, g, q * P:(q + 1) * P], w0[0:n, g, :],
                                          start=(step == 0 and q == 0), stop=(step == GROUPS - 1),
                                          skip_group_check=True)
                if step == GROUPS - 1:
                    mm.then_inc(x1_done, 1)

            def gram_block(c, buf, q, early=False):
                if q == 0:
                    pe.wait_ge(x1_copied, c + 1)
                    pe.wait_ge(diag_done, c + 1)
                if not (early and q < 2):
                    pe.wait_ge(gram_copied, BLOCKS * c + q - 1)
                nc.tensor.matmul(gram_ps[q % 2][:, 0:J * BB], x1_sb[:, q, :],
                                 spread_e[:, buf, q].rearrange("p j b -> p (j b)"),
                                 start=True, stop=True).then_inc(gram_done, 1)

            def second_layer(k, first=False):
                if not first:
                    pe.wait_ge(score_copied, k)
                pe.wait_ge(gram_copied, CHUNKS * BLOCKS * (k + 1))
                for j in range(FIELDS):
                    mm = nc.tensor.matmul(misc_ps[:, 0:P], w1_sb[:, j, :], gram[:, j, :],
                                          start=(j == 0), stop=(j == FIELDS - 1))
                mm.then_inc(z2_done, 1)

            def mlp1(k):
                pe.wait_ge(z2_copied, k + 1)
                for m in range(M1):
                    at = misc_ps[:, m * P:(m + 1) * P]
                    nc.tensor.matmul(at, wt1_sb[:, 0, m * P:(m + 1) * P], gram[:, FIELDS, :], start=True, stop=False)
                    mm = nc.tensor.matmul(at, wt1_sb[:, 1, m * P:(m + 1) * P], z2_sb[:], start=False, stop=True)
                mm.then_inc(hid1_done, 1)

            def mlp2(k):
                pe.wait_ge(hid1_ready, k + 1)
                for m in range(M2):
                    for n in range(M1):
                        mm = nc.tensor.matmul(misc_ps[:, m * P:(m + 1) * P], wt2_sb[:, n, m * P:(m + 1) * P],
                                              hid1[:, n, :], start=(n == 0), stop=(n == M1 - 1))
                mm.then_inc(hid2_done, 1)

            def mlp3(k):
                pe.wait_ge(hid2_ready, M2 * (k + 1))
                for n in range(M2):
                    mm = nc.tensor.matmul(misc_ps[0:1, 0:P], wt3_sb[:, n:n + 1], hid2[:, n, :],
                                          start=(n == 0), stop=(n == M2 - 1))
                mm.then_inc(score_done, 1)

            early_picks = {0: (0, 1), 1: (2, 3), 2: (4,), 3: (5,)}
            late_picks = {2: (0, 1), 3: (2, 3), 4: (4,), 5: (5,)}
            picks = [early_picks] * (CHUNKS - 1) + [late_picks]

            def tile(k, first=False, second=False, last=False):
                for s in range(CHUNKS):
                    c = CHUNKS * k + s
                    buf, nbuf = s % 2, (s + 1) % 2
                    nk, ns = (k + 1, 0) if s == CHUNKS - 1 else (k, s + 1)
                    grams = not (first and s == 0)
                    prepare = not (last and s == CHUNKS - 1)
                    for g in range(GROUPS):
                        sum_pairs(c, buf, g, early=first and s < 2)
                        if s == CHUNKS - 1 and prepare and g < 2:
                            turn(nk, g, used=None if first else k)
                        if grams and 1 <= g <= BLOCKS:
                            gram_block(c - 1, nbuf, g - 1, early=first and s == 1)
                        if prepare and g in picks[s]:
                            for m in picks[s][g]:
                                pick(nk, ns, c + 1, m)
                        if prepare and g == 3:
                            spread(ns, c + 1)
                        if not first:
                            if s == 1 and g == 0:
                                mlp1(k - 1)
                            if s == 2 and g == 2:
                                mlp2(k - 1)
                            if s == 3 and g == 4:
                                mlp3(k - 1)
                    if not first and s == 0:
                        second_layer(k - 1, first=second)

            dense_products(range(0, 4))
            for f in range(0, 10):
                small_field(f)
            dense_products(range(4, 8))
            for f in range(10, SMALL):
                small_field(f)
            pe.wait_ge(small_copied, 2)
            pe.wait_ge(constants_ready, 3)
            pe.wait_ge(dense_copied, 2 * M1)
            turn(0, 0, first=True)
            turn(0, 1)
            for m in range(ITEMS):
                pick(0, 0, 0, m, first=True)
            spread(0, 0, first=True)
            pe.wait_ge(w0_ready, 1)
            tile(0, first=True)
            pe.wait_ge(w1_loaded, 16)
            pe.wait_ge(mlp_loaded, 64)
            tile(1, second=True)
            with pe.Fori(2, TILES - 1) as k:
                tile(k)
            tile(TILES - 1, last=True)
            end = TILES - 1
            for q in range(BLOCKS):
                gram_block(CHUNKS * TILES - 1, (CHUNKS - 1) % 2, q)
            second_layer(end)
            mlp1(end)
            mlp2(end)
            mlp3(end)


def constants():
    import numpy as np

    c = np.zeros((P, C_ALL), np.float32)
    for part in range(PARTS):
        for r in range(R):
            for k in range(FIELDS):
                at = C_PICK + r * FIELDS + k
                for a in range(LEFTS):
                    c[part * FIELDS + (k - r - R * RIGHTS * a) % FIELDS, at + a * PAIRS] = 1
                for b in range(RIGHTS):
                    c[part * FIELDS + (k + R * b) % FIELDS, at + (LEFTS + b) * PAIRS] = 1
        for j in range(FIELDS):
            c[part * FIELDS + j, C_SPREAD + j] = 1
    c[PF, C_SPREAD + FIELDS] = 1
    c[:, C_IDENT:C_IDENT + P] = np.eye(P)
    for p in range(P):
        c[p, C_MASK + p // WIDTH] = 1
    at = C_ROWS
    for depth in DEPTHS:
        c[0:SP, at:at + depth] = np.arange(SP * depth).reshape(SP, depth)
        at += depth
    return c


def pair_fields():
    import numpy as np

    r = np.arange(PAIRS) // FIELDS
    k = np.arange(PAIRS) % FIELDS
    g = np.arange(GROUPS)[:, None]
    return (k - r - R * RIGHTS * (g // RIGHTS)) % FIELDS, (k + R * (g % RIGHTS)) % FIELDS


def kernel(**inputs):
    import numpy as np
    import concourse.bacc as bacc
    from concourse.bass_utils import run_bass_kernel_spmd

    x = {n: np.asarray(a) for n, a in inputs.items()}
    order = sorted(range(FIELDS), key=lambda f: x[f"tbl_{f}"].shape[0])
    lf, rt = pair_fields()
    used = np.arange(PAIRS)[None, :] < np.array(GROUP_ROWS)[:, None]
    w = x["L0_rec_W0"].reshape(H, FIELDS, FIELDS)[:, order][:, :, order]
    ids = x["ids"][:, order]
    w0a = np.where(used[:, :, None], w[:, lf, rt].transpose(1, 2, 0), np.float32(0)).transpose(1, 0, 2)
    w0b = np.where((used & (lf != rt))[:, :, None], w[:, rt, lf].transpose(1, 2, 0), np.float32(0)).transpose(1, 0, 2)
    arrays = {
        "ids": ids.reshape(TILES, P, FIELDS).transpose(1, 0, 2),
        "ids_small": ids[0:P, 0:SMALL].T.reshape(1, SMALL * P),
        **{f"tbl_{f}": x[f"tbl_{f}"] for f in range(FIELDS)},
        "consts": constants(),
        "w0a": w0a,
        "w0b": w0b,
        "w1": x["L0_rec_W1"].reshape(H, H, FIELDS)[:, :, order].transpose(1, 2, 0),
        "dense": x["dense_ctx"].T,
        "wt1": x["W_top1"][0:2 * H].reshape(2, H, HID1).transpose(1, 0, 2),
        "wtd": x["W_top1"][2 * H:],
        "b1": x["b_top1"].reshape(M1, P).T,
        "wt2": x["W_top2"].reshape(M1, P, HID2).transpose(1, 0, 2),
        "b2": x["b_top2"].reshape(M2, P).T,
        "wt3": x["W_top3"].reshape(M2, P).T,
    }
    nc = bacc.Bacc("TRN2", target_bir_lowering=False, num_devices=1)
    aps = {}
    for name, a in arrays.items():
        arrays[name] = np.ascontiguousarray(a)
        aps[name] = nc.dram_tensor(f"{name}_dram", a.shape, mybir.dt.from_np(a.dtype), kind="ExternalInput").ap()
    out = nc.dram_tensor("y_dram", (1, BATCH), F32, kind="ExternalOutput").ap()
    build(nc, aps["ids"], aps["ids_small"], [aps[f"tbl_{f}"] for f in order],
          *[aps[n] for n in ("consts", "w0a", "w0b", "w1", "dense", "wt1", "wtd", "b1", "wt2", "b2", "wt3")], out)
    r = run_bass_kernel_spmd(nc, [{f"{n}_dram": a for n, a in arrays.items()}], core_ids=[0])
    return r.results[0]["y_dram"].reshape(BATCH, 1)
```

```python
from contextlib import ExitStack

import concourse.bass as bass
from concourse import mybir

F32 = mybir.dt.float32
BF16 = mybir.dt.bfloat16
I32 = mybir.dt.int32
ALU = mybir.AluOpType
ACT = mybir.ActivationFunctionType

P = 128
FIELDS = 39
WIDTH = 16
BATCH = 1024
TILES = BATCH // P
CHUNKS = 4
CB = P // CHUNKS
COLS = WIDTH * CB
BLOCKS = 4
BB = CB // BLOCKS
PARTS = 3
ITEMS = 4
LEFTS = 3
MEMBERS = [(0, 1), (0, 2), (1, 2), (0, 3), (1, 3), (2, 3)]
GROUPS = len(MEMBERS)
FIRST_GROUP = [m * (m - 1) // 2 for m in range(ITEMS)]
PF = PARTS * FIELDS
J = FIELDS + 1
H = 128
HID1, HID2 = 512, 256
M1, M2 = HID1 // P, HID2 // P
HALF = WIDTH // 2
SMALL = 16
SP = 125
DEPTHS = (8, 10)
BATCHES = ((0, 4), (4, 10), (10, 16))
HOTS = 4
EARLY = 32
HALF_SMALL = SMALL // 2

C_PICK = 0
C_SPREAD = C_PICK + ITEMS * P
C_IDENT = C_SPREAD + J
C_MASK = C_IDENT + P
C_ROWS = C_MASK + BB
C_LEAVE = C_ROWS + sum(DEPTHS)
C_ALL = C_LEAVE + 2


def build(nc, ids, ids_small, tables, consts, w0a, w0b, w0_squares, w1, dense, wt1, wtd, b1, wt2, b2, wt3, out):
    depth = [t.shape[0] // SP for t in tables[0:SMALL]]
    first_slot = [sum(depth[0:f]) for f in range(SMALL + 1)]
    slots = first_slot[SMALL]
    rows_at = [sum(DEPTHS[0:DEPTHS.index(d)]) for d in depth]

    with ExitStack() as ctx:
        def sb(name, shape, dt=F32):
            return ctx.enter_context(nc.sbuf_tensor(name, shape, dt))

        def pb(name):
            return ctx.enter_context(nc.psum_tensor(name, [P, 512], F32))

        def sem(name):
            return ctx.enter_context(nc.semaphore(name))

        ids_sb = sb("ids_sb", [P, TILES, FIELDS], I32)
        rows_now = sb("rows_now", [P, 2, FIELDS], I32)
        consts_sb = sb("consts_sb", [P, C_ALL])
        consts_bf = sb("consts_bf", [P, C_MASK], BF16)
        emb = sb("emb", [P, 2, FIELDS, WIDTH])
        rest = sb("rest", [P, FIELDS, WIDTH])
        parts = sb("parts", [P, PARTS, FIELDS, WIDTH], BF16)
        cols = sb("cols", [P, P, WIDTH], BF16)
        left = sb("left", [P, LEFTS, COLS])
        pairs = sb("pairs", [P, 2, GROUPS, COLS])
        w0 = sb("w0", [P, GROUPS, H])
        w0_other = sb("w0_other", [P, GROUPS, H])
        squares = sb("squares", [P, COLS])
        squares_rest = sb("squares_rest", [P, COLS])
        squares_part = sb("squares_part", [P, 2, COLS], BF16)
        square_parts = sb("square_parts", [P, 2, COLS], BF16)
        ws = sb("ws", [P, H])
        ws_rest = sb("ws_rest", [P, H])
        ws_parts = sb("ws_parts", [P, PARTS, H], BF16)
        w1_sb = sb("w1_sb", [P, FIELDS, H])
        spread_e = sb("spread_e", [P, 2, BLOCKS, J, BB])
        x1_sb = sb("x1_sb", [P, BLOCKS, H])
        gram = sb("gram", [P, J, P])
        z2_sb = sb("z2_sb", [P, P])
        dense_sb = sb("dense_sb", [WIDTH, BATCH])
        wtd_sb = sb("wtd_sb", [WIDTH, HID1])
        dense_part = sb("dense_part", [P, M1, BATCH])
        wt1_sb = sb("wt1_sb", [P, 2, HID1])
        b1_sb = sb("b1_sb", [P, M1])
        wt2_sb = sb("wt2_sb", [P, M1, HID2])
        b2_sb = sb("b2_sb", [P, M2])
        wt3_sb = sb("wt3_sb", [P, M2])
        hid1_sum = sb("hid1_sum", [P, M1, P])
        hid1 = sb("hid1", [P, M1, P])
        hid2 = sb("hid2", [P, M2, P])
        y_sb = sb("y_sb", [1, BATCH])

        F16 = mybir.dt.float16
        gram_flat = gram[:].rearrange("p j b -> p (j b)")
        small_tab = gram_flat[:, 0:slots * WIDTH].rearrange("p (m d) -> p m d", d=WIDTH)
        small_rest = gram_flat[:, slots * WIDTH:2 * slots * WIDTH].rearrange("p (m d) -> p m d", d=WIDTH)
        pairs_flat = pairs[:].rearrange("p u g n -> p (u g n)")
        small_words = slots * PARTS * WIDTH // 2
        small_parts = pairs_flat[:, 0:small_words].bitcast(BF16).rearrange("p (m a d) -> p m a d", a=PARTS, d=WIDTH)
        ids_words = SMALL * P // 2
        ids_f16 = pairs_flat[:, small_words:small_words + ids_words].bitcast(F16).rearrange("p (f b) -> p f b", b=P)
        hot = sb("hot", [P, HOTS, max(DEPTHS), P], BF16)
        ids_rep = hot[:].rearrange("p u m b -> p (u m b)")[:, 0:2 * SMALL * P].bitcast(I32)
        spread_flat = spread_e[:].rearrange("p u q j b -> p (u q j b)")
        rows_words = sum(DEPTHS) * P // 2
        row_numbers = spread_flat[:, 0:rows_words].bitcast(F16).rearrange("p (m b) -> p m b", b=P)

        pick_ps = [pb("pick_ps0"), pb("pick_ps1")]
        x1_ps = [pb("x1_ps0"), pb("x1_ps1")]
        gram_ps = [pb("gram_ps0"), pb("gram_ps1")]
        spread_ps = pb("spread_ps")
        misc_ps = pb("misc_ps")

        ids_loaded = sem("ids_loaded")
        consts_loaded = sem("consts_loaded")
        ids_rep_loaded = sem("ids_rep_loaded")
        small_loaded = [sem(f"small_loaded{n}") for n in range(len(BATCHES))]
        small_step = sem("small_step")
        small_rested = sem("small_rested")
        hot_done = sem("hot_done")
        hot_used = sem("hot_used")
        small_copied = sem("small_copied")
        dense_loaded = sem("dense_loaded")
        w0_loaded = sem("w0_loaded")
        w1_loaded = sem("w1_loaded")
        mlp_loaded = sem("mlp_loaded")
        constants_ready = sem("constants_ready")
        w0_ready = sem("w0_ready")
        dense_done = sem("dense_done")
        dense_copied = sem("dense_copied")
        rows_ready = sem("rows_ready")
        rows_seen = sem("rows_seen")
        gathered = [sem("gathered0"), sem("gathered1")]
        gathered_early = sem("gathered_early")
        early_step = sem("early_step")
        emb_read = sem("emb_read")
        split_step = sem("split_step")
        split_done = sem("split_done")
        turned = sem("turned")
        cols_copied = sem("cols_copied")
        cols_copied_2 = sem("cols_copied_2")
        first_cols_copied = sem("first_cols_copied")
        picked = sem("picked")
        left_copied = sem("left_copied")
        pairs_done = sem("pairs_done")
        squares_step = sem("squares_step")
        squares_rested = sem("squares_rested")
        squares_done = sem("squares_done")
        ws_step = sem("ws_step")
        spread_done = sem("spread_done")
        diag_done = sem("diag_done")
        x1_done = sem("x1_done")
        x1_copied = sem("x1_copied")
        gram_done = sem("gram_done")
        gram_copied = sem("gram_copied")
        z2_done = sem("z2_done")
        z2_copied = sem("z2_copied")
        hid1_done = sem("hid1_done")
        hid1_added = sem("hid1_added")
        hid1_ready = sem("hid1_ready")
        last_hid1_ready = sem("last_hid1_ready")
        hid2_done = sem("hid2_done")
        hid2_ready = sem("hid2_ready")
        score_done = sem("score_done")
        score_copied = sem("score_copied")
        stored = sem("stored")

        block = ctx.enter_context(nc.Block())

        def turned_view(bank):
            return bank[0:PF, :].bitcast(BF16).rearrange("p (d b) -> p b d", b=P)

        @block.sync
        def _(sp):
            sp.dma_start(ids_sb[:], ids).then_inc(ids_loaded, 16)
            sp.dma_start(ids_rep, ids_small.to_broadcast([P, SMALL * P])).then_inc(ids_rep_loaded, 16)
            sp.dma_start(consts_sb[:], consts).then_inc(consts_loaded, 16)
            for n, (lo, hi) in enumerate(BATCHES):
                for f in range(lo, hi):
                    sp.dma_start(small_tab[0:SP, first_slot[f]:first_slot[f + 1], :],
                                 tables[f].rearrange("(p m) d -> p m d", p=SP)).then_inc(small_loaded[n], 16)
                if n == 0:
                    for dst, src in ((dense_sb[:], dense), (wtd_sb[:], wtd), (b1_sb[:], b1)):
                        sp.dma_start(dst, src).then_inc(dense_loaded, 16)
            for dst, src in ((w0[:], w0a), (w0_other[:], w0b), (ws[0:PF], w0_squares)):
                sp.dma_start(dst, src).then_inc(w0_loaded, 16)
            sp.dma_start(w1_sb[:], w1).then_inc(w1_loaded, 16)
            for dst, src in ((wt1_sb[:], wt1), (wt2_sb[:], wt2), (b2_sb[:], b2), (wt3_sb[:], wt3)):
                sp.dma_start(dst, src).then_inc(mlp_loaded, 16)
            sp.wait_ge(score_copied, TILES)
            sp.dma_start(out, y_sb[:]).then_inc(stored, 16)
            sp.wait_ge(stored, 16)

        @block.gpsimd
        def _(pool):
            def gather(k, parity, fields=range(FIELDS), early=0):
                nc.gpsimd.tensor_copy(rows_now[:, parity:parity + 1, :], ids_sb[:, bass.ds(k, 1), :]
                                      ).then_inc(rows_ready, 1)
                pool.wait_ge(rows_ready, k + 1)
                pool.sem_inc(rows_seen, 1)
                for f in fields:
                    pool.indirect_dma_start(
                        out=emb[:, parity, f, :], out_offset=None, in_=tables[f],
                        in_offset=bass.IndirectOffsetOnAxis(ap=rows_now[:, parity, f:f + 1], axis=0),
                    ).then_inc(gathered_early if f < early else gathered[parity], 16)

            pool.wait_ge(ids_loaded, 16)
            gather(0, 0, range(SMALL, FIELDS))
            gather(1, 1, early=EARLY)
            with pool.Fori(1, TILES // 2) as pair:
                k = 2 * pair
                pool.wait_ge(emb_read, k - 1)
                gather(k, 0)
                pool.wait_ge(emb_read, k)
                gather(k + 1, 1)

        @block.scalar
        def _(act):
            def small_batch_part(n, a):
                lo, hi = (first_slot[f] for f in BATCHES[n])
                if a == 0:
                    act.wait_ge(small_loaded[n], 16 * (BATCHES[n][1] - BATCHES[n][0]))
                else:
                    act.wait_ge(small_rested, 2 * n + 1)
                src = (small_tab, small_rest)[a]
                nc.scalar.copy(small_parts[0:SP, lo:hi, a, :], src[0:SP, lo:hi, :]).then_inc(small_step, 1)

            def copy_small(bank):
                act.wait_ge(hot_used, HALF_SMALL * (bank + 1))
                f = HALF_SMALL * bank
                nc.scalar.copy(parts[:, :, f:f + HALF_SMALL, :],
                               gram_ps[bank][:, 0:HALF_SMALL * PARTS * WIDTH].rearrange(
                                   "p (f a d) -> p a f d", a=PARTS, d=WIDTH)).then_inc(small_copied, 1)

            def copy_dense(steps):
                act.wait_ge(dense_loaded, 48)
                for n in steps:
                    m, half = n // 2, n % 2
                    act.wait_ge(dense_done, n + 1)
                    nc.scalar.activation(dense_part[:, m, half * 512:half * 512 + 512], x1_ps[n % 2][:],
                                         ACT.Identity, bias=b1_sb[:, m:m + 1]).then_inc(dense_copied, 1)

            def copy_cols(k, rows=slice(0, P), done=cols_copied):
                act.wait_ge(turned, 2 * k + 1)
                nc.scalar.copy(cols[0:PF, rows, 0:HALF], turned_view(spread_ps)[:, rows, :]).then_inc(done, 1)

            def copy_left(c, which, first=False):
                for a in which:
                    act.wait_ge(picked, ITEMS * c + a + 1)
                    if a == 0 and not first:
                        act.wait_ge(pairs_done, ITEMS * c)
                    nc.scalar.copy(left[:, a, :], pick_ps[a % 2][:]).then_inc(left_copied, 1)

            def squares_copy(c, a):
                if a == 0:
                    act.wait_ge(pairs_done, ITEMS * c + 1)
                else:
                    act.wait_ge(squares_rested, c + 1)
                nc.scalar.copy(squares_part[0:PF, a, :], (squares, squares_rest)[a][0:PF]).then_inc(squares_step, 1)

            def copy_x1(c, bank, first=False):
                act.wait_ge(x1_done, c + 1)
                if not first:
                    act.wait_ge(gram_done, BLOCKS * c)
                nc.scalar.copy(x1_sb[:], x1_ps[bank][:].rearrange("p (q i) -> p q i", i=H)
                               ).then_inc(x1_copied, 1)

            def copy_gram(k, s, q):
                act.wait_ge(gram_done, BLOCKS * (CHUNKS * k + s) + q + 1)
                b = s * CB + q * BB
                nc.scalar.copy(gram[:, :, b:b + BB],
                               gram_ps[q % 2][:, 0:J * BB].rearrange("p (j b) -> p j b", b=BB)
                               ).then_inc(gram_copied, 1)

            def copy_z2(k):
                act.wait_ge(z2_done, k + 1)
                nc.scalar.copy(z2_sb[:], misc_ps[:, 0:P]).then_inc(z2_copied, 1)

            def relu_hid1(k, first=False):
                act.wait_ge(hid1_added, k + 1)
                if not first:
                    act.wait_ge(hid2_done, k)
                nc.scalar.activation(hid1[:], hid1_sum[:], ACT.Relu).then_inc(hid1_ready, 1)

            def relu_hid2(k, first=False):
                act.wait_ge(hid2_done, k + 1)
                if not first:
                    act.wait_ge(score_done, k)
                for m in range(M2):
                    nc.scalar.activation(hid2[:, m, :], misc_ps[:, m * P:(m + 1) * P], ACT.Relu,
                                         bias=b2_sb[:, m:m + 1]).then_inc(hid2_ready, 1)

            def relu_last():
                for m in range(M1):
                    if m % 2 == 0:
                        act.wait_ge(hid1_done, TILES - 1 + m // 2 + 1)
                    nc.scalar.activation(hid1[:, m, :], x1_ps[m // 2][:, m % 2 * P:(m % 2 + 1) * P], ACT.Relu,
                                         bias=b1_sb[:, m:m + 1]).then_inc(last_hid1_ready, 1)
                for m in range(M2):
                    act.wait_ge(hid2_done, TILES - 1 + m + 1)
                    nc.scalar.activation(hid2[:, m, :], gram_ps[m][:, 0:P], ACT.Relu,
                                         bias=b2_sb[:, m:m + 1]).then_inc(hid2_ready, 1)

            def copy_score(k):
                act.wait_ge(score_done, k + 1)
                nc.scalar.copy(y_sb[:, bass.ds(k * P, P)], misc_ps[0:1, 0:P]).then_inc(score_copied, 1)

            def tile(k, first=False, second=False, last=False):
                for s in range(CHUNKS):
                    c = CHUNKS * k + s
                    grams = not (first and s == 0)
                    gk, gs = (k - 1, CHUNKS - 1) if s == 0 else (k, s - 1)
                    if grams:
                        copy_x1(c - 1, gs % 2, first=first and s == 1)
                    if s == 1 and not first:
                        act.wait_ge(hid1_done, k)
                    if s == 2 and not first:
                        relu_hid1(k - 1, first=second)
                    if s < 3:
                        copy_left(c + 1, (0, 1))
                        squares_copy(c + 1, 0)
                        for q in range(BLOCKS):
                            if q == 2:
                                squares_copy(c + 1, 1)
                                copy_left(c + 1, (2,))
                            if grams:
                                copy_gram(gk, gs, q)
                            if s == 2 and q == 2 and not first:
                                relu_hid2(k - 1, first=second)
                        if s == 0 and not first:
                            copy_z2(k - 1)
                    elif last:
                        for q in range(BLOCKS):
                            copy_gram(gk, gs, q)
                    else:
                        copy_cols(k + 1)
                        before = 2 if first else 1
                        for q in range(before):
                            copy_gram(gk, gs, q)
                        copy_left(c + 1, (0, 1))
                        squares_copy(c + 1, 0)
                        for q in range(before, BLOCKS):
                            copy_gram(gk, gs, q)
                        squares_copy(c + 1, 1)
                        copy_left(c + 1, (2,))
                    if s == 3 and not first:
                        copy_score(k - 1)

            act.wait_ge(ids_rep_loaded, 16)
            nc.scalar.copy(ids_f16, ids_rep.rearrange("p (f b) -> p f b", b=P)).then_inc(small_step, 1)
            act.wait_ge(consts_loaded, 16)
            nc.scalar.copy(row_numbers, consts_sb[:, C_ROWS:C_LEAVE, None].to_broadcast([P, sum(DEPTHS), P])
                           ).then_inc(small_step, 1)
            small_batch_part(0, 0)
            small_batch_part(0, 1)
            copy_dense(range(0, 2))
            small_batch_part(1, 0)
            copy_dense(range(2, 4))
            small_batch_part(1, 1)
            small_batch_part(2, 0)
            copy_dense(range(4, 5))
            small_batch_part(2, 1)
            copy_dense(range(5, 7))
            copy_small(0)
            copy_small(1)
            copy_dense(range(7, 8))
            act.wait_ge(constants_ready, 3)
            copy_cols(0, slice(0, CB), first_cols_copied)
            copy_cols(0, slice(CB, P))
            copy_left(0, (0, 1), first=True)
            squares_copy(0, 0)
            squares_copy(0, 1)
            copy_left(0, (2,), first=True)
            act.wait_ge(mlp_loaded, 64)
            tile(0, first=True)
            tile(1, second=True)
            with act.Fori(2, TILES - 1) as k:
                tile(k)
            tile(TILES - 1, last=True)
            end = TILES - 1
            copy_x1(CHUNKS * TILES - 1, (CHUNKS - 1) % 2)
            for q in range(BLOCKS):
                copy_gram(end, CHUNKS - 1, q)
            copy_z2(end)
            relu_last()
            copy_score(end)

        @block.vector
        def _(dve):
            def split(k, parity, at=0):
                e, rest_e, part = emb[:, parity, at:, :], rest[:, at:, :], parts[:, 0, at:, :]
                dve.wait_ge(gathered[parity], 8 * FIELDS * (k + 2 - parity) - 16 * (SMALL, EARLY)[parity])
                if at != SMALL:
                    dve.wait_ge(turned, 2 * k)
                nc.vector.tensor_copy(part, e).then_inc(split_step, 1)
                dve.wait_ge(split_step, 2 * k + 1)
                nc.vector.tensor_tensor(rest_e, e, part, ALU.subtract).then_inc(emb_read, 1)

            def split_rest(k, at=0):
                rest_e, part = rest[:, at:, :], [parts[:, a, at:, :] for a in range(PARTS)]
                dve.wait_ge(emb_read, k + 1)
                nc.vector.tensor_copy(part[1], rest_e).then_inc(split_step, 1)
                dve.wait_ge(split_step, 2 * k + 2)
                nc.vector.tensor_tensor(part[2], rest_e, part[1], ALU.subtract).then_inc(split_done, 1)

            def split_early():
                e, rest_e, part = emb[:, 1, 0:EARLY, :], rest[:, 0:EARLY, :], [parts[:, a, 0:EARLY, :] for a in range(PARTS)]
                dve.wait_ge(gathered_early, 16 * EARLY)
                dve.wait_ge(turned, 2)
                nc.vector.tensor_copy(part[0], e).then_inc(early_step, 1)
                dve.wait_ge(early_step, 1)
                nc.vector.tensor_tensor(rest_e, e, part[0], ALU.subtract).then_inc(early_step, 1)
                dve.wait_ge(early_step, 2)
                nc.vector.tensor_copy(part[1], rest_e).then_inc(early_step, 1)
                dve.wait_ge(early_step, 3)
                nc.vector.tensor_tensor(part[2], rest_e, part[1], ALU.subtract).then_inc(early_step, 1)

            def small_rests(n, step):
                lo, hi = (first_slot[f] for f in BATCHES[n])
                rest_n, tab_n = small_rest[0:SP, lo:hi, :], small_tab[0:SP, lo:hi, :]
                part = [small_parts[0:SP, lo:hi, a, :] for a in range(PARTS)]
                dve.wait_ge(small_step, 2 + 2 * n + step + 1)
                if step == 0:
                    dve.wait_ge(small_loaded[n], 16 * (BATCHES[n][1] - BATCHES[n][0]))
                    nc.vector.tensor_tensor(rest_n, tab_n, part[0], ALU.subtract).then_inc(small_rested, 1)
                else:
                    nc.vector.tensor_tensor(part[2], rest_n, part[1], ALU.subtract).then_inc(small_rested, 1)

            def one_hot(f):
                if f >= HOTS:
                    dve.wait_ge(hot_used, f - HOTS + 1)
                nc.vector.tensor_tensor(hot[0:SP, f % HOTS, 0:depth[f], :],
                                        ids_f16[0:SP, f:f + 1, :].to_broadcast([SP, depth[f], P]),
                                        row_numbers[0:SP, rows_at[f]:rows_at[f] + depth[f], :],
                                        ALU.is_equal).then_inc(hot_done, 1)

            def copy_cols(k, rows=slice(0, P), done=cols_copied_2):
                dve.wait_ge(turned, 2 * k + 2)
                nc.vector.tensor_copy(cols[0:PF, rows, HALF:WIDTH], turned_view(misc_ps)[:, rows, :]).then_inc(done, 1)

            def multiply(c, buf, m):
                dve.wait_ge(picked, ITEMS * c + m + 1)
                dve.wait_ge(left_copied, LEFTS * c + min(m + 1, LEFTS))
                if m == 0:
                    nc.vector.tensor_tensor(squares[:], pick_ps[0][:], left[:, 0, :], ALU.mult).then_inc(pairs_done, 1)
                else:
                    at = FIRST_GROUP[m]
                    nc.vector.tensor_tensor(pairs[:, buf, at:at + m, :],
                                            pick_ps[m % 2][:, None, :].to_broadcast([P, m, COLS]),
                                            left[:, 0:m, :], ALU.mult).then_inc(pairs_done, 1)

            def squares_leave(c, first=False):
                dve.wait_ge(squares_step, 2 * c + 1)
                if not first:
                    dve.wait_ge(squares_done, c)
                nc.vector.scalar_tensor_tensor(squares_rest[0:PF], squares_part[0:PF, 0, :],
                                               consts_sb[0:PF, C_LEAVE:C_LEAVE + 1], squares[0:PF],
                                               ALU.mult, ALU.add).then_inc(squares_rested, 1)

            def squares_place(c, buf):
                dve.wait_ge(squares_step, 2 * c + 2)
                nc.vector.scalar_tensor_tensor(square_parts[0:PF, buf, :], squares_part[0:PF, 1, :],
                                               consts_sb[0:PF, C_LEAVE + 1:C_LEAVE + 2], squares_rest[0:PF],
                                               ALU.mult, ALU.add).then_inc(squares_done, 1)

            def split_ws():
                nc.vector.tensor_copy(ws_parts[0:PF, 0, :], ws[0:PF]).then_inc(ws_step, 1)
                dve.wait_ge(ws_step, 1)
                nc.vector.tensor_tensor(ws_rest[0:PF], ws[0:PF], ws_parts[0:PF, 0, :], ALU.subtract).then_inc(ws_step, 1)
                dve.wait_ge(ws_step, 2)
                nc.vector.tensor_copy(ws_parts[0:PF, 1, :], ws_rest[0:PF]).then_inc(ws_step, 1)
                dve.wait_ge(ws_step, 3)
                nc.vector.tensor_tensor(ws_parts[0:PF, 2, :], ws_rest[0:PF], ws_parts[0:PF, 1, :], ALU.subtract
                                        ).then_inc(ws_step, 1)

            def diagonal(c, buf, first=False):
                dve.wait_ge(spread_done, c + 1)
                if not first:
                    dve.wait_ge(gram_done, BLOCKS * (c - 1))
                e = spread_ps[:, 0:BLOCKS * J].rearrange("p (q j) -> p q j", j=J)
                nc.vector.tensor_tensor(
                    spread_e[:, buf], e[:, :, :, None].to_broadcast([P, BLOCKS, J, BB]),
                    consts_sb[:, None, None, C_MASK:C_ROWS].to_broadcast([P, BLOCKS, J, BB]),
                    ALU.mult).then_inc(diag_done, 1)

            def add_hid1(k):
                dve.wait_ge(hid1_done, k + 1)
                nc.vector.tensor_tensor(hid1_sum[:], misc_ps[:].rearrange("p (m b) -> p m b", b=P),
                                        dense_part[:, :, bass.ds(k * P, P)], ALU.add).then_inc(hid1_added, 1)

            def finish(c, buf, first=False):
                squares_place(c, buf)
                diagonal(c, buf, first=first)

            def chunk_0(k, early=False):
                c = CHUNKS * k
                if not early:
                    dve.wait_ge(x1_done, c - 1)
                for m in range(ITEMS):
                    multiply(c, 0, m)
                    if m == 1:
                        squares_leave(c, first=early)

            def tile(k, parity, first=False, second=False, last=False):
                for s in range(CHUNKS - 1):
                    c, buf = CHUNKS * k + s + 1, (s + 1) % 2
                    if s == 1 and not first:
                        add_hid1(k - 1)
                    if not (first and s == 0):
                        dve.wait_ge(x1_done, c - 1)
                    multiply(c, buf, 0)
                    multiply(c, buf, 1)
                    if s == 0:
                        finish(c - 1, 1 - buf, first=first)
                    squares_leave(c)
                    if s == 2 and first:
                        split_early()
                    if s == (2 if second else 1) and not first and not last:
                        split(k + 1, 1 - parity)
                    if s == 2 and not first and not last:
                        split_rest(k + 1)
                    multiply(c, buf, 2)
                    if s == 2 and first:
                        diagonal(c, buf)
                        split(k + 1, 1 - parity, at=EARLY)
                        split_rest(k + 1, at=EARLY)
                        multiply(c, buf, 3)
                        squares_place(c, buf)
                    else:
                        multiply(c, buf, 3)
                        finish(c, buf, first=first and s == 0)
                if not last:
                    copy_cols(k + 1)
                    chunk_0(k + 1)

            nc.vector.memset(cols[96:P], 1.0).then_inc(constants_ready, 2)
            dve.wait_ge(consts_loaded, 16)
            nc.vector.tensor_copy(consts_bf[:], consts_sb[:, 0:C_MASK]).then_inc(constants_ready, 1)
            for n, (lo, hi) in enumerate(BATCHES):
                small_rests(n, 0)
                for f in range(lo, lo + 2):
                    one_hot(f)
                small_rests(n, 1)
                for f in range(lo + 2, hi):
                    one_hot(f)
            split(0, 0, at=SMALL)
            split_rest(0, at=SMALL)
            dve.wait_ge(w0_loaded, 48)
            nc.vector.tensor_tensor(w0[:], w0[:], w0_other[:], ALU.add).then_inc(w0_ready, 1)
            split_ws()
            dve.wait_ge(small_copied, 2)
            copy_cols(0, slice(0, CB), first_cols_copied)
            copy_cols(0, slice(CB, P))
            chunk_0(0, early=True)
            tile(0, 0, first=True)
            dve.wait_ge(dense_copied, 2 * M1)
            tile(1, 1, second=True)
            with dve.Fori(1, TILES // 2 - 1) as pair:
                k = 2 * pair
                tile(k, 0)
                tile(k + 1, 1)
            tile(TILES - 2, 0)
            tile(TILES - 1, 1, last=True)

        @block.tensor
        def _(pe):
            def small_field(f):
                batch = next(n for n, (lo, hi) in enumerate(BATCHES) if lo <= f < hi)
                if f == BATCHES[batch][0]:
                    pe.wait_ge(small_rested, 2 * batch + 2)
                pe.wait_ge(hot_done, f + 1)
                at = f % HALF_SMALL * PARTS * WIDTH
                for m in range(depth[f]):
                    mm = nc.tensor.matmul(gram_ps[f // HALF_SMALL][:, at:at + PARTS * WIDTH],
                                          hot[0:SP, f % HOTS, m, :],
                                          small_parts[0:SP, first_slot[f] + m, :, :].rearrange("p a d -> p (a d)"),
                                          start=(m == 0), stop=(m == depth[f] - 1))
                mm.then_inc(hot_used, 1)

            def dense_products(steps):
                pe.wait_ge(dense_loaded, 48)
                for n in steps:
                    m, half = n // 2, n % 2
                    if n >= 2:
                        pe.wait_ge(dense_copied, n - 1)
                    nc.tensor.matmul(x1_ps[n % 2][:], wtd_sb[:, m * P:(m + 1) * P],
                                     dense_sb[:, half * 512:half * 512 + 512],
                                     start=True, stop=True).then_inc(dense_done, 1)

            def turn(k, half, first=False, used=None, early=False):
                if half == 0:
                    pe.wait_ge(split_done, k + 1)
                    if early:
                        pe.wait_ge(early_step, 4)
                    if not first:
                        pe.wait_ge(diag_done, CHUNKS * k)
                elif used is not None:
                    pe.wait_ge(hid2_ready, M2 * used)
                out_ps = (spread_ps, misc_ps)[half][0:PF, :].bitcast(BF16)
                for n in range(HALF):
                    mm = nc.tensor.transpose(out_ps[:, n * P:(n + 1) * P],
                                             parts[:, :, :, half * HALF + n].rearrange("p a f -> p (a f)"),
                                             consts_bf[:, C_IDENT:C_IDENT + P])
                mm.then_inc(turned, 1)

            def spread(s, c, first=False):
                if not first:
                    pe.wait_ge(diag_done, c)
                for q in range(BLOCKS):
                    b = s * CB + q * BB
                    mm = nc.tensor.matmul(spread_ps[:, q * J:(q + 1) * J],
                                          cols[0:PF + 1, b:b + BB, :].rearrange("p b d -> p (b d)"),
                                          consts_bf[0:PF + 1, C_SPREAD:C_SPREAD + J], start=True, stop=True)
                mm.then_inc(spread_done, 1)

            def pick(k, s, c, m, first=False, after_first=False):
                if m == 0 and first:
                    pe.wait_ge(first_cols_copied, 2)
                elif m == 0 and (s == 0 or after_first):
                    pe.wait_ge(cols_copied, k + 1)
                    pe.wait_ge(cols_copied_2, k + 1)
                if m >= 2 or not first:
                    pe.wait_ge(pairs_done, ITEMS * c + m - 1)
                at = C_PICK + m * P
                nc.tensor.matmul(pick_ps[m % 2][:], consts_bf[0:PF, at:at + P],
                                 cols[0:PF, s * CB:(s + 1) * CB, :], start=True, stop=True).then_inc(picked, 1)

            def sum_pairs(c, buf, g, early=False):
                if g in FIRST_GROUP[1:]:
                    pe.wait_ge(pairs_done, ITEMS * c + FIRST_GROUP.index(g, 1) + 1)
                if g == 0 and not early:
                    pe.wait_ge(x1_copied, c - 1)
                for q in range(BLOCKS):
                    mm = nc.tensor.matmul(x1_ps[buf][:, q * H:(q + 1) * H],
                                          pairs[:, buf, g, q * P:(q + 1) * P], w0[:, g, :],
                                          start=(g == 0 and q == 0), stop=False,
                                          skip_group_check=True)

            def sum_squares(c, buf):
                pe.wait_ge(squares_done, c + 1)
                for q in range(BLOCKS):
                    for a in range(PARTS):
                        mm = nc.tensor.matmul(x1_ps[buf][:, q * H:(q + 1) * H],
                                              square_parts[0:PF, buf, q * P:(q + 1) * P], ws_parts[0:PF, a, :],
                                              start=False, stop=(a == PARTS - 1), skip_group_check=True)
                mm.then_inc(x1_done, 1)

            def gram_block(c, buf, q, early=False):
                if q == 0:
                    pe.wait_ge(x1_copied, c + 1)
                    pe.wait_ge(diag_done, c + 1)
                if not (early and q < 2):
                    pe.wait_ge(gram_copied, BLOCKS * c + q - 1)
                nc.tensor.matmul(gram_ps[q % 2][:, 0:J * BB], x1_sb[:, q, :],
                                 spread_e[:, buf, q].rearrange("p j b -> p (j b)"),
                                 start=True, stop=True).then_inc(gram_done, 1)

            def second_layer(k, first=False):
                if not first:
                    pe.wait_ge(score_copied, k)
                pe.wait_ge(gram_copied, CHUNKS * BLOCKS * (k + 1))
                for j in range(FIELDS):
                    mm = nc.tensor.matmul(misc_ps[:, 0:P], w1_sb[:, j, :], gram[:, j, :],
                                          start=(j == 0), stop=(j == FIELDS - 1))
                mm.then_inc(z2_done, 1)

            def mlp1(k):
                pe.wait_ge(z2_copied, k + 1)
                for m in range(M1):
                    at = misc_ps[:, m * P:(m + 1) * P]
                    nc.tensor.matmul(at, wt1_sb[:, 0, m * P:(m + 1) * P], gram[:, FIELDS, :], start=True, stop=False)
                    mm = nc.tensor.matmul(at, wt1_sb[:, 1, m * P:(m + 1) * P], z2_sb[:], start=False, stop=True)
                mm.then_inc(hid1_done, 1)

            def mlp2(k):
                pe.wait_ge(hid1_ready, k + 1)
                for m in range(M2):
                    for n in range(M1):
                        mm = nc.tensor.matmul(misc_ps[:, m * P:(m + 1) * P], wt2_sb[:, n, m * P:(m + 1) * P],
                                              hid1[:, n, :], start=(n == 0), stop=(n == M1 - 1))
                mm.then_inc(hid2_done, 1)

            def last_mlp():
                end = TILES - 1
                at = [x1_ps[m // 2][:, m % 2 * P:(m % 2 + 1) * P] for m in range(M1)]
                cut = [slice(m * P, (m + 1) * P) for m in range(M1)]
                for m in range(M1):
                    nc.tensor.matmul(at[m], wtd_sb[:, cut[m]], dense_sb[:, end * P:], start=(m % 2 == 0), stop=False,
                                     skip_group_check=True)
                for m in range(M1):
                    nc.tensor.matmul(at[m], wt1_sb[:, 0, cut[m]], gram[:, FIELDS, :], start=False, stop=False,
                                     skip_group_check=True)
                pe.wait_ge(z2_copied, end + 1)
                for m in range(M1):
                    mm = nc.tensor.matmul(at[m], wt1_sb[:, 1, cut[m]], z2_sb[:], start=False, stop=True,
                                          skip_group_check=True)
                    if m % 2 == 1:
                        mm.then_inc(hid1_done, 1)
                for m in range(M2):
                    for n in range(M1):
                        if m == 0:
                            pe.wait_ge(last_hid1_ready, n + 1)
                        mm = nc.tensor.matmul(gram_ps[m][:, 0:P], wt2_sb[:, n, cut[m]], hid1[:, n, :],
                                              start=(n == 0), stop=(n == M1 - 1))
                    mm.then_inc(hid2_done, 1)

            def mlp3(k):
                pe.wait_ge(hid2_ready, M2 * (k + 1))
                for n in range(M2):
                    mm = nc.tensor.matmul(misc_ps[0:1, 0:P], wt3_sb[:, n:n + 1], hid2[:, n, :],
                                          start=(n == 0), stop=(n == M2 - 1))
                mm.then_inc(score_done, 1)

            early_picks = {0: (0,), 1: (1,), 2: (2,), 3: (3,)}
            late_picks = {2: (0, 1), 3: (2,), 4: (3,)}
            first_late_picks = {3: (0, 1), 4: (2,), 5: (3,)}

            def tile(k, first=False, second=False, last=False):
                for s in range(CHUNKS):
                    c = CHUNKS * k + s
                    buf, nbuf = s % 2, (s + 1) % 2
                    nk, ns = (k + 1, 0) if s == CHUNKS - 1 else (k, s + 1)
                    grams = not (first and s == 0)
                    prepare = not (last and s == CHUNKS - 1)
                    picks = early_picks if s < CHUNKS - 1 else first_late_picks if first else late_picks
                    for g in range(GROUPS):
                        sum_pairs(c, buf, g, early=first and s < 2)
                        half = g - 1 if first else g
                        if s == CHUNKS - 1 and prepare and half in (0, 1):
                            turn(nk, half, used=None if first else k, early=first)
                        if grams and 1 <= g <= BLOCKS:
                            gram_block(c - 1, nbuf, g - 1, early=first and s == 1)
                        for m in picks.get(g, ()) if prepare else ():
                            pick(nk, ns, c + 1, m, after_first=first and s == 0)
                        if prepare and g == (4 if s == 0 else 3):
                            spread(ns, c + 1)
                        if not first:
                            if s == 1 and g == 0:
                                mlp1(k - 1)
                            if s == 2 and g == 2:
                                mlp2(k - 1)
                            if s == 3 and g == 4:
                                mlp3(k - 1)
                    if first and s == 0:
                        pe.wait_ge(ws_step, 4)
                    sum_squares(c, buf)
                    if not first and s == 0:
                        second_layer(k - 1, first=second)

            dense_products(range(0, 4))
            for f in range(0, 4):
                small_field(f)
            dense_products(range(4, 5))
            for f in range(4, 10):
                small_field(f)
            dense_products(range(5, 7))
            for f in range(10, SMALL):
                small_field(f)
            dense_products(range(7, 8))
            pe.wait_ge(small_copied, 2)
            pe.wait_ge(constants_ready, 3)
            turn(0, 0, first=True)
            turn(0, 1)
            for m in range(ITEMS):
                pick(0, 0, 0, m, first=True)
            pe.wait_ge(cols_copied, 1)
            spread(0, 0, first=True)
            pe.wait_ge(dense_copied, 2 * M1)
            pe.wait_ge(w0_ready, 1)
            tile(0, first=True)
            pe.wait_ge(w1_loaded, 16)
            pe.wait_ge(mlp_loaded, 64)
            tile(1, second=True)
            with pe.Fori(2, TILES - 1) as k:
                tile(k)
            tile(TILES - 1, last=True)
            end = TILES - 1
            for q in range(BLOCKS):
                gram_block(CHUNKS * TILES - 1, (CHUNKS - 1) % 2, q)
            second_layer(end)
            last_mlp()
            mlp3(end)


def quads():
    n = FIELDS - 3
    u = (n, n + 1, n + 2)
    first = [[] for _ in range(FIELDS)]
    others = []
    for t in range(n):
        first[t].append((t, (t + 2) % n, (t + 10) % n, (t + 17) % n))
        first[t].append((t, (t + 3) % n, (t + 14) % n, (t + 23) % n))
        if t < 9:
            first[u[t % 3]].append((u[t % 3], t, (t + 1) % n, (t + 5) % n))
        else:
            first[t].append((t, u[t % 3], (t + 1) % n, (t + 5) % n))
    for t in range(6):
        first[t].append((t, t + 6, t + 12, t + 18))
        (first[t + 6] if t < 3 else others).append((t + 6, t, t + 24, t + 30))
        others.append((t + 12, t + 18, t + 24, t + 30))
    others.append((u[0], u[1], u[2], 0))
    others.append(others[0])
    sets = [first[f][part] for part in range(PARTS) for f in range(FIELDS)] + others
    assert len(sets) == P
    return sets


def constants():
    import numpy as np

    c = np.zeros((P, C_ALL), np.float32)
    for part in range(PARTS):
        for row, fields in enumerate(quads()):
            for m, f in enumerate(fields):
                c[part * FIELDS + f, C_PICK + m * P + row] = 1
        for j in range(FIELDS):
            c[part * FIELDS + j, C_SPREAD + j] = 1
    c[PF, C_SPREAD + FIELDS] = 1
    c[:, C_IDENT:C_IDENT + P] = np.eye(P)
    for p in range(P):
        c[p, C_MASK + p // WIDTH] = 1
    c[FIELDS:PF, C_LEAVE] = -1
    c[2 * FIELDS:PF, C_LEAVE + 1] = -1
    at = C_ROWS
    for depth in DEPTHS:
        c[0:SP, at:at + depth] = np.arange(SP * depth).reshape(SP, depth)
        at += depth
    return c


def pair_fields():
    import numpy as np

    q = np.array(quads())
    left = np.stack([q[:, a] for a, _ in MEMBERS])
    right = np.stack([q[:, b] for _, b in MEMBERS])
    used = np.zeros(left.shape, bool)
    seen = set()
    for g in range(GROUPS):
        for row in range(P):
            pair = frozenset((left[g, row], right[g, row]))
            used[g, row] = pair not in seen
            seen.add(pair)
    assert len(seen) == FIELDS * (FIELDS - 1) // 2
    return left, right, used


def kernel(**inputs):
    import numpy as np
    import concourse.bacc as bacc
    from concourse.bass_utils import run_bass_kernel_spmd

    x = {n: np.asarray(a) for n, a in inputs.items()}
    order = sorted(range(FIELDS), key=lambda f: x[f"tbl_{f}"].shape[0])
    lf, rt, used = pair_fields()
    w = x["L0_rec_W0"].reshape(H, FIELDS, FIELDS)[:, order][:, :, order]
    ids = x["ids"][:, order]
    w0a = np.where(used[:, :, None], w[:, lf, rt].transpose(1, 2, 0), np.float32(0)).transpose(1, 0, 2)
    w0b = np.where(used[:, :, None], w[:, rt, lf].transpose(1, 2, 0), np.float32(0)).transpose(1, 0, 2)
    arrays = {
        "ids": ids.reshape(TILES, P, FIELDS).transpose(1, 0, 2),
        "ids_small": ids[0:P, 0:SMALL].T.reshape(1, SMALL * P),
        **{f"tbl_{f}": x[f"tbl_{f}"] for f in range(FIELDS)},
        "consts": constants(),
        "w0a": w0a,
        "w0b": w0b,
        "w0_squares": np.tile(w.diagonal(axis1=1, axis2=2).T, (PARTS, 1)),
        "w1": x["L0_rec_W1"].reshape(H, H, FIELDS)[:, :, order].transpose(1, 2, 0),
        "dense": x["dense_ctx"].T,
        "wt1": x["W_top1"][0:2 * H].reshape(2, H, HID1).transpose(1, 0, 2),
        "wtd": x["W_top1"][2 * H:],
        "b1": x["b_top1"].reshape(M1, P).T,
        "wt2": x["W_top2"].reshape(M1, P, HID2).transpose(1, 0, 2),
        "b2": x["b_top2"].reshape(M2, P).T,
        "wt3": x["W_top3"].reshape(M2, P).T,
    }
    nc = bacc.Bacc("TRN2", target_bir_lowering=False, num_devices=1)
    aps = {}
    for name, a in arrays.items():
        arrays[name] = np.ascontiguousarray(a)
        aps[name] = nc.dram_tensor(f"{name}_dram", a.shape, mybir.dt.from_np(a.dtype), kind="ExternalInput").ap()
    out = nc.dram_tensor("y_dram", (1, BATCH), F32, kind="ExternalOutput").ap()
    build(nc, aps["ids"], aps["ids_small"], [aps[f"tbl_{f}"] for f in order],
          *[aps[n] for n in ("consts", "w0a", "w0b", "w0_squares", "w1", "dense", "wt1", "wtd", "b1", "wt2", "b2", "wt3")], out)
    r = run_bass_kernel_spmd(nc, [{f"{n}_dram": a for n, a in arrays.items()}], core_ids=[0])
    return r.results[0]["y_dram"].reshape(BATCH, 1)
```
